# Optimizing a Trainium2 kernel written in Bass

```python
import numpy as np
import jax
import jax.numpy as jnp

def _softmax(x, axis=-1):
    return jax.nn.softmax(x, axis=axis)

def _gelu(x):
    return jax.nn.gelu(x, approximate=True)

def _silu(x):
    return jax.nn.silu(x)

def _sigmoid(x):
    return jax.nn.sigmoid(x)

def _layernorm(x, axis=-1, eps=1e-05):
    m = jnp.mean(x, axis=axis, keepdims=True)
    v = jnp.var(x, axis=axis, keepdims=True)
    return (x - m) / jnp.sqrt(v + eps)

def _scatter_add(tgt, idx, src, axis=0):
    return tgt.at[idx].add(src)

def _segment_sum(src, seg, n):
    return jax.ops.segment_sum(src, seg, n)
kernel_name = 'mk_lm_tower_d1_tok_ids512_r4_4ccd8a'

def setup_inputs(seed: int=0):
    np.random.seed(seed)
    _w = jnp.asarray

    def _rec_inputs():
        import jax
        import jax.numpy as jnp
        _rk = jax.random.key(seed)
        x = jax.random.randint(jax.random.fold_in(_rk, 1), (8, 1024), 0, 64, jnp.int32)
        return x
    x = _rec_inputs()

    def _L0_tok_setup():
        import jax, jax.numpy as jnp
        import numpy as np
        NGRAM_SIZES = (2, 3, 4)
        HASH_VOCAB = 25000
        EMBED_DIM = 128
        BATCH, SEQ = (8, 1024)

        def _ngram_hash_ids(byte_sequence, n):
            L = byte_sequence.shape[1] - n + 1
            h = jnp.zeros((byte_sequence.shape[0], L), dtype=jnp.int64)
            for j in range(n):
                h = (h * 64 + byte_sequence[:, j:j + L]) % HASH_VOCAB
            return h

        def _ngram_embed(byte_sequence, table, n):
            B, S = byte_sequence.shape
            ids = _ngram_hash_ids(byte_sequence, n)
            emb = table[ids]
            out = jnp.zeros((B, S, table.shape[1]), dtype=table.dtype)
            c = n // 2
            return out.at[:, c:c + emb.shape[1]].set(emb)
        key = jax.random.key(seed)
        ks = jax.random.split(key, 6)
        return {'byte_sequence': jax.random.randint(ks[0], (BATCH, SEQ), 0, 64, dtype=jnp.int64), 'emb_2': jax.random.normal(ks[1], (HASH_VOCAB, EMBED_DIM), dtype=jnp.float32), 'emb_3': jax.random.normal(ks[2], (HASH_VOCAB, EMBED_DIM), dtype=jnp.float32), 'emb_4': jax.random.normal(ks[3], (HASH_VOCAB, EMBED_DIM), dtype=jnp.float32), 'proj_w': jax.random.normal(ks[4], (EMBED_DIM, len(NGRAM_SIZES) * EMBED_DIM), dtype=jnp.float32) * 0.02, 'proj_b': jax.random.normal(ks[5], (EMBED_DIM,), dtype=jnp.float32) * 0.02}
    _L0_tok_all = _L0_tok_setup()
    _L0_tok_in = {k: v for k, v in _L0_tok_all.items() if k in ('emb_2', 'emb_3', 'emb_4', 'proj_w', 'proj_b')}
    del _L0_tok_all

    def _L0_attn_setup():
        import jax, jax.numpy as jnp
        import numpy as np
        ALPHA, LR, DECAY = (0.1, 0.01, 0.9)
        CHUNK = 64

        def _gelu(x):
            return jax.nn.gelu(x, approximate=False)

        def _mem(k, W0, W1):
            return _gelu(k @ W0) @ W1
        key = jax.random.key(seed)
        ks = jax.random.split(key, 6)
        D, H = (128, 256)
        B, S = (4, 2048)

        def xavier(k, shape):
            lim = float(np.sqrt(6.0 / (shape[0] + shape[1])))
            return jax.random.uniform(k, shape, jnp.float32, -lim, lim)
        return {'x': jax.random.normal(ks[0], (B, S, D), jnp.float32), 'w_k': xavier(ks[1], (D, D)), 'w_v': xavier(ks[2], (D, D)), 'w_q': xavier(ks[3], (D, D)), 'W0': xavier(ks[4], (D, H)), 'W1': xavier(ks[5], (H, D))}
    _L0_attn_all = _L0_attn_setup()
    _L0_attn_in = {k: v for k, v in _L0_attn_all.items() if k in ('w_k', 'w_v', 'w_q', 'W0', 'W1')}
    del _L0_attn_all

    def _L0_ffn_setup():
        import jax, jax.numpy as jnp
        import numpy as np
        import math
        B, T, D, H, E, TOPK = (8, 1024, 128, 512, 8, 2)
        CAP_FRAC = 1.0

        def _expert_ffn(x, w1, w2, w3):
            h = jax.nn.gelu(x @ w2 * (x @ w1), approximate=False)
            return h @ w3
        key = jax.random.key(seed)
        ks = jax.random.split(key, 6)
        x = jax.random.normal(ks[0], (B, T, D), dtype=jnp.float32)
        Wr = jax.random.normal(ks[1], (D, E), dtype=jnp.float32) * 0.02
        br = jnp.zeros((E,), dtype=jnp.float32)
        W1 = jax.random.normal(ks[2], (E, D, H), dtype=jnp.float32) * 0.02
        W2 = jax.random.normal(ks[3], (E, D, H), dtype=jnp.float32) * 0.02
        W3 = jax.random.normal(ks[4], (E, H, D), dtype=jnp.float32) * 0.02
        return {'x': x, 'Wr': Wr, 'br': br, 'W1': W1, 'W2': W2, 'W3': W3}
    _L0_ffn_all = _L0_ffn_setup()
    _L0_ffn_in = {k: v for k, v in _L0_ffn_all.items() if k in ('Wr', 'br', 'W1', 'W2', 'W3')}
    del _L0_ffn_all
    return {'x': x, 'L0_tok_emb_2': _L0_tok_in['emb_2'], 'L0_tok_emb_3': _L0_tok_in['emb_3'], 'L0_tok_emb_4': _L0_tok_in['emb_4'], 'L0_tok_proj_w': _L0_tok_in['proj_w'], 'L0_tok_proj_b': _L0_tok_in['proj_b'], 'L0_attn_w_k': _L0_attn_in['w_k'], 'L0_attn_w_v': _L0_attn_in['w_v'], 'L0_attn_w_q': _L0_attn_in['w_q'], 'L0_attn_W0': _L0_attn_in['W0'], 'L0_attn_W1': _L0_attn_in['W1'], 'L0_ffn_Wr': _L0_ffn_in['Wr'], 'L0_ffn_br': _L0_ffn_in['br'], 'L0_ffn_W1': _L0_ffn_in['W1'], 'L0_ffn_W2': _L0_ffn_in['W2'], 'L0_ffn_W3': _L0_ffn_in['W3']}

def reference(x, L0_tok_emb_2, L0_tok_emb_3, L0_tok_emb_4, L0_tok_proj_w, L0_tok_proj_b, L0_attn_w_k, L0_attn_w_v, L0_attn_w_q, L0_attn_W0, L0_attn_W1, L0_ffn_Wr, L0_ffn_br, L0_ffn_W1, L0_ffn_W2, L0_ffn_W3):
    import jax
    import jax.numpy as jnp

    def _L0_tok_ref(byte_sequence, emb_2, emb_3, emb_4, proj_w, proj_b):
        import jax, jax.numpy as jnp
        import numpy as np
        NGRAM_SIZES = (2, 3, 4)
        HASH_VOCAB = 25000
        EMBED_DIM = 128
        BATCH, SEQ = (8, 1024)

        def _ngram_hash_ids(byte_sequence, n):
            L = byte_sequence.shape[1] - n + 1
            h = jnp.zeros((byte_sequence.shape[0], L), dtype=jnp.int64)
            for j in range(n):
                h = (h * 64 + byte_sequence[:, j:j + L]) % HASH_VOCAB
            return h

        def _ngram_embed(byte_sequence, table, n):
            B, S = byte_sequence.shape
            ids = _ngram_hash_ids(byte_sequence, n)
            emb = table[ids]
            out = jnp.zeros((B, S, table.shape[1]), dtype=table.dtype)
            c = n // 2
            return out.at[:, c:c + emb.shape[1]].set(emb)
        tables = (emb_2, emb_3, emb_4)
        combined = jnp.concatenate([_ngram_embed(byte_sequence, t, n) for t, n in zip(tables, NGRAM_SIZES)], axis=-1)
        return jnp.einsum('bsk,dk->bsd', combined, proj_w) + proj_b

    def _L0_attn_ref(x, w_k, w_v, w_q, W0, W1):
        import jax, jax.numpy as jnp
        import numpy as np
        ALPHA, LR, DECAY = (0.1, 0.01, 0.9)
        CHUNK = 64

        def _gelu(x):
            return jax.nn.gelu(x, approximate=False)

        def _mem(k, W0, W1):
            return _gelu(k @ W0) @ W1
        B, S, D = x.shape
        nc = S // CHUNK
        chunks = x.reshape(B, nc, CHUNK, D).swapaxes(0, 1)

        def loss_fn(Ws, k, v):
            return jnp.mean((_mem(k, Ws[0], Ws[1]) - v) ** 2)
        grad_fn = jax.grad(loss_fn)

        def step(surp, chunk):
            k = chunk @ w_k
            v = chunk @ w_v
            g0, g1 = grad_fn((W0, W1), k, v)
            s0 = DECAY * jax.lax.stop_gradient(surp[0]) - LR * g0
            s1 = DECAY * jax.lax.stop_gradient(surp[1]) - LR * g1
            return ((s0, s1), None)
        init = (jnp.zeros_like(W0), jnp.zeros_like(W1))
        (s0, s1), _ = jax.lax.scan(step, init, chunks)
        fw0 = (1.0 - ALPHA) * W0 + s0
        fw1 = (1.0 - ALPHA) * W1 + s1
        q = x @ w_q
        return _mem(q, fw0, fw1)

    def _L0_ffn_ref(x, Wr, br, W1, W2, W3):
        import jax, jax.numpy as jnp
        import numpy as np
        import math
        B, T, D, H, E, TOPK = (8, 1024, 128, 512, 8, 2)
        CAP_FRAC = 1.0

        def _expert_ffn(x, w1, w2, w3):
            h = jax.nn.gelu(x @ w2 * (x @ w1), approximate=False)
            return h @ w3
        b, t, d = x.shape
        Bt = b * t
        x_flat = x.reshape(Bt, d)
        logits = x_flat.astype(jnp.float32) @ Wr + br
        vals, idx = jax.lax.top_k(logits, TOPK)
        scores = jax.nn.softmax(vals, axis=-1).astype(x.dtype).reshape(b, t, TOPK)
        onehot = jax.nn.one_hot(idx, E, dtype=jnp.float32)
        pos = jnp.cumsum(jnp.cumsum(onehot, axis=0), axis=1).astype(jnp.int32)
        capacity = math.floor(Bt * CAP_FRAC)
        mask3 = onehot * (pos < capacity)
        token_mask = mask3.sum(-1).reshape(b, t, TOPK)
        assign = jnp.einsum('tke,e->tk', mask3, jnp.arange(E, dtype=jnp.float32)).astype(jnp.int32)
        i_max = assign.reshape(b, t, TOPK).max(axis=-1)
        y = jnp.zeros_like(x)
        for i in range(E):
            yi = _expert_ffn(x, W1[i], W2[i], W3[i])
            y = jnp.where((i_max == i)[..., None], yi, y)
        expert_outputs = jnp.where(token_mask[..., None] > 0, y[:, :, None, :], x[:, :, None, :])
        return jnp.einsum('btkD,btk->btD', expert_outputs, scores)
    h = _L0_tok_ref(x, L0_tok_emb_2, L0_tok_emb_3, L0_tok_emb_4, L0_tok_proj_w, L0_tok_proj_b)
    h = h + _L0_attn_ref(_layernorm(h, axis=-1), L0_attn_w_k, L0_attn_w_v, L0_attn_w_q, L0_attn_W0, L0_attn_W1)
    h = h + _L0_ffn_ref(_layernorm(h, axis=-1), L0_ffn_Wr, L0_ffn_br, L0_ffn_W1, L0_ffn_W2, L0_ffn_W3)
    return h

_drawn_inputs = setup_inputs


def setup_inputs(seed=0):
    import zlib

    import numpy as np

    out = dict(_drawn_inputs(seed))
    spreads = {'L0_ffn_br': (0.0, 0.435)}
    factors = {'L0_attn_w_k': 8.0,
     'L0_attn_w_v': 8.0,
     'L0_ffn_Wr': 3.416,
     'L0_ffn_W1': 3.035,
     'L0_ffn_W2': 3.041,
     'L0_ffn_W3': 3.028}
    for name, (base, spread) in spreads.items():
        noise = np.random.default_rng([zlib.crc32(name.encode()), seed]).standard_normal(out[name].shape)
        drawn = base * np.exp(spread * noise) if base else spread * noise
        out[name] = jnp.asarray(drawn.astype(out[name].dtype))
    for name, factor in factors.items():
        out[name] = (out[name] * factor).astype(out[name].dtype)
    return out
```

```python
import math
from contextlib import ExitStack

import concourse.bass as bass
from concourse import mybir

P = 128
BATCH, SEQ = 8, 1024
TOK = BATCH * SEQ
D = 128
H = 256
F = 512
E = 8
NGRAM = 3
VOCAB = 25000
CHUNK = 64
NCHUNK = SEQ // CHUNK
NT = TOK // P
GT = 4
GTOK = GT * P
NG = TOK // GTOK
GPS = SEQ // GTOK
NS = NT + E - 1
ROW = 132
RSTD, NMR, SCORE = 128, 129, 130
RING = 8
LAG = 5
ALPHA, LR, DECAY = 0.1, 0.01, 0.9
EPS = 1e-5
TINY = 2.0 ** -60
GRAD = -LR * 2.0 / (BATCH * CHUNK * D)
MAGIC = float(0x5F3759DF)
SKIP = float(1 << 20)
BIG = 3.0e38


def wait(eng, sem, value):
    if isinstance(value, int) and value <= 0:
        return
    eng.wait_ge(sem, value)


def tower(nc, x, emb2, emb3, emb4, proj_w, proj_b, w_k, w_v, w_q, W0, W1, Wr, br, F1, F2, F3, out):
    f32, bf16, i32 = mybir.dt.float32, mybir.dt.bfloat16, mybir.dt.int32
    ALU, ACT, AX = mybir.AluOpType, mybir.ActivationFunctionType, mybir.AxisListType.X
    tables = [emb2, emb3, emb4]
    ctx = ExitStack()
    with ctx:
        def sb(name, shape, dt=f32):
            return ctx.enter_context(nc.sbuf_tensor(name, shape, dt))

        def sem(name):
            return ctx.enter_context(nc.semaphore(name))

        colf = sb("colf", [P, P])
        rowf = sb("rowf", [P, 1])
        ident = sb("ident", [P, P])
        before = sb("before", [P, P], bf16)
        ones_bf = sb("ones_bf", [P, P], bf16)
        tilef = sb("tilef", [P, NT])
        decay = sb("decay", [P, GPS, GT])
        lastp = sb("lastp", [P, 1])
        tiny_c = sb("tiny_c", [P, 1])
        rowp1 = sb("rowp1", [P, 1])
        proj_s = sb("proj_s", [P, NGRAM * D])
        projT = sb("projT", [P, NGRAM, D])
        bias_bc = sb("bias_bc", [P, D])
        br_bc = sb("br_bc", [P, E])
        wk_s, wv_s, wq_s = sb("wk_s", [P, D]), sb("wv_s", [P, D]), sb("wq_s", [P, D])
        wkT, wqT, nwv = sb("wkT", [P, D]), sb("wqT", [P, D]), sb("nwv", [P, D])
        w0_s = sb("w0_s", [P, H])
        w1_s = sb("w1_s", [P, 2, D])
        w1T = sb("w1T", [P, H])
        wkz = sb("wkz", [P, H])
        g0raw = sb("g0raw", [P, H])
        g1T = sb("g1T", [P, H])
        fw0 = sb("fw0", [P, H])
        fw1 = sb("fw1", [P, 2, D])
        wqz = sb("wqz", [P, H])
        wr_s = sb("wr_s", [P, E])
        f1_s = sb("f1_s", [P, E, F])
        f2_s = sb("f2_s", [P, E, F])
        f3_s = sb("f3_s", [P, E, 4, D])
        f1_f, f2_f = (t[:].rearrange("p e f -> p (e f)") for t in (f1_s, f2_s))
        f3_f = f3_s[:].rearrange("p e c d -> p (e c d)")
        rows = sb("rows", [P, NT, ROW])
        xnF_all = sb("xnF_all", [P, TOK])
        rowsf = rows[:].rearrange("p j c -> p (j c)")
        logits = sb("logits", [P, NT, E])
        work = sb("work", [P, 16384])
        at = [0]

        def carve(cols, dt=f32):
            a = at[0]
            at[0] += cols
            assert at[0] <= 16384, at[0]
            v = work[:, a:a + cols]
            return v if dt is f32 else v.bitcast(dt)

        gath = [carve(NGRAM * GTOK).rearrange("p (n t d) -> p n t d", n=NGRAM, t=GT) for _ in range(2)]
        embF = [carve(NGRAM * GTOK).rearrange("p (n c) -> p n c", n=NGRAM) for _ in range(2)]
        xnT = [carve(GTOK).rearrange("p (t d) -> p t d", t=GT) for _ in range(2)]
        xnF = [carve(GTOK) for _ in range(2)]
        act_t = carve(GT * H)
        act_f = carve(2 * GTOK)
        zsq, rz2, ez = (carve(GT * H) for _ in range(3))
        lnz = rz2
        num = carve(GT * H)
        dz = carve(GT * H)
        res_t = carve(GTOK)
        res_f = sb("res_f", [P, GTOK])
        idx_all = sb("idx_all", [P, NGRAM, NT], i32)
        idx_g = [sb(f"idx_g{k}", [P, NGRAM, GT], i32) for k in range(2)]
        stats, mv = sb("stats", [P, GT, 6]), sb("mv", [P, GT, 2])
        ve, seed, ya, yb, rstd = (sb(n, [P, GT]) for n in ("ve", "seed", "ya", "yb", "rstd"))
        nmr = sb("nmr", [P, GT])
        at[0] = 0
        act2 = [carve(2 * GTOK) for _ in range(2)]
        x2t = carve(GTOK).rearrange("p (t d) -> p t d", t=GT)
        x2f = carve(GTOK)
        fE = NT * E
        big3 = lambda v: v.rearrange("p (j e) -> p j e", e=E)
        iota_e = big3(carve(fE))
        eqm, cand, lg2 = big3(carve(fE)), big3(carve(fE)), big3(carve(fE))
        oh0, oh1, ohm = (big3(carve(fE // 2, bf16)) for _ in range(3))
        incl, base = big3(carve(fE)), big3(carve(fE))
        m1, m2, t0, t1, imax, ex, den, s0, s1, pos = (carve(NT) for _ in range(10))
        slot_a, slot_b = carve(NT), carve(NT)
        pos_i, a_i, b_i = (carve(NT, i32) for _ in range(3))
        ones_f = carve(NT)
        full0, full1, k0, k1, kk, cx = carve(E), carve(E), carve(1), carve(1), carve(E), carve(1)
        nt_f, nt_i, nt_c, first = carve(E), carve(E, i32), carve(E), carve(E)
        starts = carve(NS * E).rearrange("p (a e) -> p a e", e=E)
        tile_e = carve(NS)
        oh_b = xnF_all[:, 0:NT * P // 2].bitcast(bf16).rearrange("p (j b) -> p j b", b=P)
        NSP = NS + 1
        oh_a = xnF_all[:, 4096:4096 + NT * NSP // 2].bitcast(bf16).rearrange("p (j a) -> p j a", a=NSP)
        val_a = work[:, 9216:9216 + NT * NSP].bitcast(bf16).rearrange("p (j v a) -> p j v a", v=2, a=NSP)
        assert at[0] <= 9216
        slot_v = sb("slot_v", [P, NSP])
        val0 = sb("val0", [P, NSP])
        slot_idx = sb("slot_idx", [P, NSP, 2], i32)
        slot_if = slot_idx[:].rearrange("p a v -> p (a v)")
        exp_idx = sb("exp_idx", [P, NSP], i32)
        at[0] = 0
        got = [sb(f"got{k}", [P, ROW]) for k in range(RING)]
        idx_s = [sb(f"idx_s{k}", [P, 2], i32) for k in range(RING)]
        xg = [carve(P) for _ in range(2)]
        xgF = [carve(P) for _ in range(2)]
        u1s = [carve(F) for _ in range(2)]
        hid = [carve(F) for _ in range(2)]
        act_e = [carve(F) for _ in range(2)]
        act_eF = [carve(F) for _ in range(2)]
        outs = [carve(P) for _ in range(2)]
        HW = P + 3
        at[0] = 0
        xw = carve(HW, i32)[0:NT]
        hb, h2, h3, h4, vv, rr, tt = (carve(HW)[0:NT] for _ in range(7))
        qi = carve(HW, i32)[0:NT]
        pz = ctx.enter_context(nc.psum_tensor("pz", [P, 1024], f32))
        pa = ctx.enter_context(nc.psum_tensor("pa", [P, 1024], f32))
        pe_ = [ctx.enter_context(nc.psum_tensor(f"pe{k}", [P, 512], f32)) for k in range(2)]
        ph = ctx.enter_context(nc.psum_tensor("ph", [P, 512], f32))
        pg = ctx.enter_context(nc.psum_tensor("pg", [P, 512], f32))
        rows_d = nc.dram_tensor("rows_d", (TOK, ROW), f32).ap()

        s_x, s_w, s_f, s_row = sem("x_loaded"), sem("weights_loaded"), sem("experts_loaded"), sem("rows_stored")
        s_const, s_pool0, s_hz = sem("constants_made"), sem("iotas_made"), sem("x_zeroed")
        s_hstep, s_hash = sem("hash_step"), sem("hashes_made")
        s_hT, s_idx = sem("hashes_transposed"), sem("indices_made")
        s_wT, s_wTs, s_wkz, s_wkzs = sem("weights_transposed"), sem("weight_copies"), sem("wkz_in_psum"), sem("wkz_made")
        s_icopy = [sem(f"group_indices{k}") for k in range(2)]
        s_gath = [[sem(f"gathered{k}_{n}") for n in range(NGRAM)] for k in range(2)]
        s_eT = [sem(f"embedding_transposed{n}") for n in range(NGRAM)]
        s_eF = [sem(f"embedding_copied{n}") for n in range(NGRAM)]
        s_h0, s_h0s = sem("h0_in_psum"), sem("h0_copied")
        s_bn, s_ag, s_nw, s_xn = sem("stats_made"), sem("stats_joined"), sem("newton_step"), sem("normed")
        s_xT, s_xF, s_xall = sem("normed_transposed"), sem("normed_copied"), [sem(f"normed_kept{k}") for k in range(2)]
        s_z, s_act, s_sq, s_ln, s_r, s_e = (sem(n) for n in ("z_in_psum", "gelu_made", "z_squared", "log_made", "inverse_made", "exp_made"))
        s_aT, s_aF = sem("gelu_transposed"), sem("gelu_copied")
        s_m, s_res, s_rT, s_rF, s_g1 = (sem(n) for n in ("residual_in_psum", "residual_made", "residual_transposed", "residual_copied", "grad1_added"))
        s_n1, s_n2, s_n3, s_gp = (sem(n) for n in ("gz_made", "phi_made", "ez_made", "slope_made"))
        s_da, s_dz, s_g0 = sem("da_in_psum"), sem("dz_made"), sem("grad0_added")
        s_gz = sem("gradients_zeroed")
        s_up, s_ups = sem("update_in_psum"), sem("update_copied")
        s_q, s_a2, s_h1, s_h1s = sem("zq_in_psum"), sem("gelu2_made"), sem("h1_in_psum"), sem("h1_copied")
        s_ag2n = sem("negated_mean_made")
        s_bn2, s_ag2, s_nw2, s_xn2 = sem("stats2_made"), sem("stats2_joined"), sem("newton2_step"), sem("normed2")
        s_x2T, s_x2F, s_lg, s_lgs = (sem(n) for n in ("normed2_transposed", "normed2_copied", "logits_in_psum", "logits_copied"))
        s_rt, s_top, s_rtact, s_cnt, s_rank, s_ohm, s_rows = (sem(n) for n in (
            "route_step", "top_two_found", "score_exp", "choices_counted", "ranks_in_psum", "choice_ready", "rows_ready"))
        s_onehot, s_slots, s_table = sem("one_hots_made"), sem("slots_in_psum"), sem("slot_table_made")
        s_is = sem("slot_indices_copied")
        s_got = [sem(f"rows_gathered{k}") for k in range(RING)]
        s_put = [sem(f"rows_scattered{k}") for k in range(2)]
        s_xg, s_xgT, s_xgF = sem("expert_in_normed"), sem("expert_in_transposed"), sem("expert_in_copied")
        s_u, s_u1, s_hid, s_ea, s_eaT, s_eaF = (sem(n) for n in ("up_in_psum", "up1_copied", "hidden_made", "expert_gelu", "expert_gelu_transposed", "expert_gelu_copied"))
        s_y, s_o = sem("expert_out_in_psum"), sem("expert_out_made")

        def alone(eng, sem, value):
            if not isinstance(value, int):
                value = eng.to_reg(value)
            eng.wait_ge(s_const, 1)
            eng.wait_ge(sem, value)

        NSTEP = 12
        block = ctx.enter_context(nc.Block())

        def in_pairs(eng, body):
            body(0, True, False)
            with eng.Fori(1, NG // 2 - 1) as i:
                body(i, False, False)
            body(NG // 2 - 1, False, True)

        def in_rings(eng, body):
            n = (NS + RING - 1) // RING
            body(0, True, False)
            with eng.Fori(1, n - 1) as i:
                body(i, False, False)
            body(n - 1, False, True)

        @block.sync
        def _(sp):
            xt = x.rearrange("b (j p) -> (b j) p", p=P)
            sp.wait_ge(s_hz, 1)
            sp.dma_start(xw[:, 2:2 + P], xt).then_inc(s_x, 16)
            sp.dma_start(xw[1:NT, 0:2], xt[0:NT - 1, P - 2:P]).then_inc(s_x, 16)
            sp.dma_start(xw[0:NT - 1, 2 + P:3 + P], xt[1:NT, 0:1], allow_slow_non_contiguous=True).then_inc(s_x, 16)
            for dst, src in ((proj_s[:], proj_w), (wk_s[:], w_k), (wv_s[:], w_v), (wq_s[:], w_q), (w0_s[:], W0),
                             (w1_s[:], W1.rearrange("(c p) d -> p c d", p=P)), (wr_s[:], Wr),
                             (bias_bc[:], proj_b[None, :].to_broadcast([P, D])),
                             (br_bc[:], br[None, :].to_broadcast([P, E]))):
                sp.dma_start(dst, src).then_inc(s_w, 16)
            sp.dma_start(f1_s[:], F1.rearrange("e p f -> p e f")).then_inc(s_f, 16)
            sp.dma_start(f2_s[:], F2.rearrange("e p f -> p e f")).then_inc(s_f, 16)
            sp.dma_start(f3_s[:], F3.rearrange("e (c p) d -> p e c d", p=P)).then_inc(s_f, 16)

            def keep(i, first, last):
                for par in range(2):
                    g = 2 * i + par
                    sp.wait_ge(s_xF, g + 1)
                    sp.dma_start(xnF_all[:, bass.ds(g * GTOK, GTOK)], xnF[par]).then_inc(s_xall[par], 16)
            in_pairs(sp, keep)
            sp.wait_ge(s_rows, 1)
            sp.dma_start(rows_d.rearrange("(j p) c -> p j c", p=P), rows[:]).then_inc(s_row, 16)

        @block.gpsimd
        def _(pool):
            nc.gpsimd.memset(xw[:], 0).then_inc(s_hz, 1)
            nc.gpsimd.iota(colf[:], pattern=[[1, P]], base=0, channel_multiplier=0,
                           allow_small_or_imprecise_dtypes=True).then_inc(s_pool0, 1)
            nc.gpsimd.iota(rowf[:], pattern=[[0, 1]], base=0, channel_multiplier=1,
                           allow_small_or_imprecise_dtypes=True).then_inc(s_pool0, 1)
            nc.gpsimd.iota(tilef[:], pattern=[[1, NT]], base=0, channel_multiplier=0,
                           allow_small_or_imprecise_dtypes=True).then_inc(s_pool0, 1)
            pool.wait_ge(s_idx, 1)

            def gathers(i, first, last):
                for par in range(2):
                    g = 2 * i + par
                    for n in range(NGRAM):
                        wait(pool, s_eT[n], g - 1)
                    nc.gpsimd.tensor_copy(idx_g[par][:], idx_all[:, :, bass.ds(g * GT, GT)]).then_inc(s_icopy[par], 1)
                    alone(pool, s_icopy[par], i + 1)
                    for n in range(NGRAM):
                        for t in range(GT):
                            nc.gpsimd.indirect_dma_start(
                                out=gath[par][:, n, t, :], out_offset=None, in_=tables[n],
                                in_offset=bass.IndirectOffsetOnAxis(ap=idx_g[par][:, n, t:t + 1], axis=0),
                            ).then_inc(s_gath[par][n], 16)
            in_pairs(pool, gathers)

            pool.wait_ge(s_lgs, NG)
            nc.gpsimd.iota(iota_e, pattern=[[0, NT], [1, E]], base=0, channel_multiplier=0,
                           allow_small_or_imprecise_dtypes=True).then_inc(s_pool0, 1)
            nc.gpsimd.iota(starts, pattern=[[1, NS], [0, E]], base=0, channel_multiplier=0,
                           allow_small_or_imprecise_dtypes=True).then_inc(s_pool0, 1)
            pool.wait_ge(s_table, 1)
            pool.wait_ge(s_row, 16)

            def gather(a, k, i):
                if not (isinstance(a, int) and a < RING):
                    pool.wait_ge(s_put[k % 2], 16 * ((a - RING) // 2 + 1) if isinstance(a, int)
                                 else 16 * (i * (RING // 2) + (k - RING) // 2 + 1))
                nc.gpsimd.tensor_copy(idx_s[k][:], slot_if[:, bass.ds(2 * a, 2)]).then_inc(s_is, 1)
                alone(pool, s_is, a + 1)
                nc.gpsimd.indirect_dma_start(
                    out=got[k][:], out_offset=None, in_=rows_d,
                    in_offset=bass.IndirectOffsetOnAxis(ap=idx_s[k][:, 0:1], axis=0)).then_inc(s_got[k], 16)

            def scatter(a, k):
                alone(pool, s_o, a + 1)
                nc.gpsimd.indirect_dma_start(
                    out=out.rearrange("b s d -> (b s) d"), in_=outs[k % 2],
                    out_offset=bass.IndirectOffsetOnAxis(ap=idx_s[k][:, 1:2], axis=0), in_offset=None,
                    bounds_check=TOK - 1, oob_is_err=False).then_inc(s_put[k % 2], 16)

            def move(i, first, last):
                for k in range(RING):
                    a = RING * i + k
                    if not (last and a >= NS):
                        gather(a, k, i)
                    if not (first and k < LAG):
                        scatter(a - LAG, (k - LAG) % RING)
            in_rings(pool, move)
            n = (NS + RING - 1) // RING
            for a in range(n * RING - LAG, NS):
                scatter(a, a % RING)
            for par in range(2):
                pool.wait_ge(s_put[par], 16 * ((NS - par + 1) // 2))

        @block.scalar
        def _(act):
            act.wait_ge(s_w, 16 * 9)
            nc.scalar.mul(nwv[:], wv_s[:], -1.0).then_inc(s_wTs, 1)
            act.wait_ge(s_wT, 1)
            nc.scalar.copy(projT[:], pz[:, 0:NGRAM * D].rearrange("p (n d) -> p n d", n=NGRAM)).then_inc(s_wTs, 1)
            nc.scalar.copy(wkT[:], pa[:, 0:D]).then_inc(s_wTs, 1)
            nc.scalar.copy(wqT[:], pa[:, D:2 * D]).then_inc(s_wTs, 1)
            nc.scalar.copy(w1T[:], pa[:, 2 * D:2 * D + H]).then_inc(s_wTs, 1)
            act.wait_ge(s_wkz, 1)
            nc.scalar.copy(wkz[:], ph[:, 0:H]).then_inc(s_wkzs, 1)

            def emb_copy(g, par, n):
                lo = (0 if par else 1 if n < 2 else 2)
                hi = GTOK - (1 if par and n > 0 else 0)
                act.wait_ge(s_eT[n], g + 1)
                wait(act, s_h0, g - 1)
                nc.scalar.copy(embF[par][:, n, lo:hi], pe_[(NGRAM * par + n) % 2][:, lo:hi]).then_inc(s_eF[n], 1)

            def normed_copy(g, par, i):
                act.wait_ge(s_xT, g + 1)
                wait(act, s_m, g - 1)
                wait(act, s_xall[par], 16 * i)
                nc.scalar.copy(xnF[par], ph[:]).then_inc(s_xF, 1)

            act.wait_ge(s_const, 1)
            emb_copy(0, 0, 0)
            emb_copy(0, 0, 2)
            normed_copy(0, 0, 0)

            def slot(g, par, i, has_next):
                act.wait_ge(s_z, g + 1)
                wait(act, s_aT, g)
                wait(act, s_g1, g)
                nc.scalar.activation(act_t, pz[:], ACT.Gelu).then_inc(s_act, 1)
                if has_next:
                    emb_copy(g + 1, 1 - par, 0)
                    emb_copy(g + 1, 1 - par, 2)
                act.wait_ge(s_aT, g + 1)
                wait(act, s_m, g)
                nc.scalar.copy(act_f, pa[:]).then_inc(s_aF, 1)
                act.wait_ge(s_n1, g + 1)
                nc.scalar.activation(zsq, pz[:], ACT.Square).then_inc(s_sq, 1)
                act.wait_ge(s_sq, g + 1)
                wait(act, s_gp, g)
                nc.scalar.activation(lnz, zsq, ACT.Ln, bias=tiny_c[:]).then_inc(s_ln, 1)
                act.wait_ge(s_ln, g + 1)
                nc.scalar.activation(rz2, lnz, ACT.Exp, scale=-1.0).then_inc(s_r, 1)
                nc.scalar.activation(ez, zsq, ACT.Exp, scale=-0.5).then_inc(s_e, 1)
                if has_next:
                    normed_copy(g + 1, 1 - par, i if par == 0 else i + 1)

            def memory(i, first, last):
                slot(2 * i, 0, i, True)
                slot(2 * i + 1, 1, i, not last)
            in_pairs(act, memory)

            pq = [pz, pa]

            def x2_copy(g):
                act.wait_ge(s_x2T, g + 1)
                wait(act, s_lg, g)
                nc.scalar.copy(x2f, pe_[0][:]).then_inc(s_x2F, 1)

            def recall(i, first, last):
                for par in range(2):
                    g = 2 * i + par
                    act.wait_ge(s_q, g + 1)
                    wait(act, s_h1, g - 1)
                    nc.scalar.activation(act2[par], pq[par][:], ACT.Gelu).then_inc(s_a2, 1)
                    if not (first and par == 0):
                        x2_copy(g - 1)
            in_pairs(act, recall)
            x2_copy(NG - 1)
            act.wait_ge(s_top, 1)
            nc.scalar.activation(ex, den, ACT.Exp).then_inc(s_rtact, 1)

            act.wait_ge(s_table, 1)

            def norm_rows(a, k, turn):
                act.wait_ge(s_got[k], 16 * (turn + 1))
                wait(act, s_xgT, a - 1)
                nc.scalar.activation(xg[k % 2], got[k][:, 0:D], ACT.Identity, bias=got[k][:, NMR:NMR + 1],
                                     scale=got[k][:, RSTD:RSTD + 1]).then_inc(s_xg, 1)

            norm_rows(0, 0, 0)

            def experts(i, first, last):
                for k in range(RING):
                    a = RING * i + k
                    if last and a >= NS:
                        continue
                    act.wait_ge(s_u, 2 * a + 1)
                    wait(act, s_hid, a - 1)
                    nc.scalar.copy(u1s[k % 2], (pz, pa)[k % 2][:, 0:F]).then_inc(s_u1, 1)
                    if not (last and a + 1 >= NS):
                        norm_rows(a + 1, (k + 1) % RING, i + (k + 1) // RING)
                    act.wait_ge(s_hid, a + 1)
                    wait(act, s_eaT, a - 1)
                    nc.scalar.activation(act_e[k % 2], hid[k % 2], ACT.Gelu).then_inc(s_ea, 1)
            in_rings(act, experts)

        @block.vector
        def _(dve):
            v = nc.vector
            steps = {}

            def link(ins, s):
                steps[s] = steps.get(s, 0) + 1
                ins.then_inc(s, 1)
                dve.wait_ge(s, steps[s])

            dve.wait_ge(s_pool0, 3)
            v.tensor_scalar(ident[:], colf[:], rowf[:], None, ALU.is_equal)
            v.tensor_scalar(before[:], colf[:], rowf[:], None, ALU.is_gt)
            v.tensor_scalar(lastp[:], rowf[:], float(P - 1), None, ALU.is_equal)
            v.memset(ones_bf[:], 1.0)
            v.memset(tiny_c[:], TINY)
            v.tensor_scalar(rowp1[:], rowf[:], 1.0, None, ALU.add)
            for h in range(GPS):
                for t in range(GT):
                    for half in range(2):
                        c = (h * GT + t) * (P // CHUNK) + half
                        v.memset(decay[half * CHUNK:(half + 1) * CHUNK, h, t:t + 1], GRAD * DECAY ** (NCHUNK - 1 - c))
            v.memset(rows[:, :, SCORE + 1:ROW], 0.0)
            for par in range(2):
                for n in range(NGRAM):
                    lo, hi = (0, 2 if n == 2 else 1) if par == 0 else (GTOK - 1, GTOK)
                    if par == 0 or n > 0:
                        ins = v.memset(embF[par][:, n, lo:hi], 0.0)
            ins.then_inc(s_const, 1)

            def mod(dst, src, done=s_hstep):
                link(v.tensor_scalar(qi, src, 1.0 / VOCAB, None, ALU.mult), s_hstep)
                link(v.scalar_tensor_tensor(rr, qi, -float(VOCAB), src, ALU.mult, ALU.add), s_hstep)
                link(v.tensor_scalar(tt, rr, 0.0, float(VOCAB), ALU.is_lt, ALU.mult), s_hstep)
                link(v.tensor_tensor(rr, rr, tt, ALU.add), s_hstep)
                link(v.tensor_scalar(tt, rr, float(VOCAB), -float(VOCAB), ALU.is_ge, ALU.mult), s_hstep)
                link(v.tensor_tensor(dst, rr, tt, ALU.add), done)

            dve.wait_ge(s_x, 48)
            link(v.tensor_copy(vv, xw), s_hstep)
            mod(hb, vv)
            prev = hb
            for cur in (h2, h3, h4):
                link(v.tensor_copy(vv[:, 0:1], prev[:, 0:1]), s_hstep)
                link(v.scalar_tensor_tensor(vv[:, 1:HW], prev[:, 0:HW - 1], 64.0, hb[:, 1:HW], ALU.mult, ALU.add), s_hstep)
                mod(cur, vv, s_hash if cur is h4 else s_hstep)
                prev = cur
            dve.wait_ge(s_hT, 1)
            v.tensor_copy(idx_all[:], pg[:, 0:NGRAM * NT].rearrange("p (n j) -> p n j", n=NGRAM)).then_inc(s_idx, 1)

            def newton(dst, g, s):
                k = [0]

                def step(ins):
                    k[0] += 1
                    ins.then_inc(s, 1)
                    dve.wait_ge(s, g * NSTEP + k[0])
                step(v.tensor_scalar(ve[:], mv[:, :, 1], EPS, None, ALU.add))
                step(v.tensor_scalar(seed[:].bitcast(i32), ve[:].bitcast(i32), 1, None, ALU.arith_shift_right))
                step(v.tensor_scalar(rstd[:].bitcast(i32), seed[:].bitcast(i32), -1.0, MAGIC, ALU.mult, ALU.add))
                for r in range(3):
                    step(v.scalar_tensor_tensor(ya[:], rstd[:], -0.5, ve[:], ALU.mult, ALU.mult))
                    step(v.tensor_tensor(yb[:], ya[:], rstd[:], ALU.mult))
                    step(v.scalar_tensor_tensor(rstd[:], yb[:], 1.5, rstd[:], ALU.add, ALU.mult))
                assert k[0] == NSTEP

            def bn(g, s_in, s_a, s_b):
                alone(dve, s_in, g + 1)
                for t in range(GT):
                    ins = v.bn_stats(stats[:, t, :], rowsf[:, bass.ds((g * GT + t) * ROW, D)])
                ins.then_inc(s_a, 1)
                alone(dve, s_a, g + 1)
                for t in range(GT):
                    ins = v.bn_aggr(mv[:, t, :], stats[:, t, :])
                ins.then_inc(s_b, 1)
                dve.wait_ge(s_b, g + 1)

            def emb_copy(g, par):
                lo, hi = (1, GTOK) if par == 0 else (0, GTOK - 1)
                dve.wait_ge(s_eT[1], g + 1)
                wait(dve, s_h0, g - 1)
                v.tensor_copy(embF[par][:, 1, lo:hi], pe_[(NGRAM * par + 1) % 2][:, lo:hi]).then_inc(s_eF[1], 1)

            def h0_rows(g):
                dve.wait_ge(s_h0, g + 1)
                v.tensor_tensor(rows[:, bass.ds(g * GT, GT), 0:D], ph[:].rearrange("p (t d) -> p t d", t=GT),
                                bias_bc[:].unsqueeze(1).to_broadcast([P, GT, D]), ALU.add).then_inc(s_h0s, 1)
                bn(g, s_h0s, s_bn, s_ag)

            def norm(g, par):
                newton(rstd, g, s_nw)
                wait(dve, s_g0, g - 1)
                for t in range(GT):
                    ins = v.tensor_scalar(xnT[par][:, t, :], rowsf[:, bass.ds((g * GT + t) * ROW, D)],
                                          mv[:, t, 0:1], rstd[:, t:t + 1], ALU.subtract, ALU.mult)
                ins.then_inc(s_xn, 1)

            dve.wait_ge(s_w, 16 * 9)
            emb_copy(0, 0)
            h0_rows(0)
            norm(0, 0)
            zv = pz[:]

            def slot(g, par, has_next):
                if has_next:
                    emb_copy(g + 1, 1 - par)
                dve.wait_ge(s_act, g + 1)
                wait(dve, s_dz, g)
                v.tensor_tensor(num, act_t, zv, ALU.mult).then_inc(s_n1, 1)
                if has_next:
                    h0_rows(g + 1)
                dve.wait_ge(s_m, g + 1)
                wait(dve, s_rT, g)
                wait(dve, s_g1, g)
                v.tensor_tensor(res_t.rearrange("p (t d) -> p t d", t=GT),
                                pa[:, 0:GTOK].rearrange("p (t d) -> p t d", t=GT),
                                decay[:, par, :].unsqueeze(2).to_broadcast([P, GT, D]), ALU.mult).then_inc(s_res, 1)
                if has_next:
                    norm(g + 1, 1 - par)
                dve.wait_ge(s_rT, g + 1)
                wait(dve, s_da, g)
                v.tensor_copy(res_f[:], pa[:, GTOK:2 * GTOK]).then_inc(s_rF, 1)
                dve.wait_ge(s_n1, g + 1)
                dve.wait_ge(s_r, g + 1)
                v.scalar_tensor_tensor(num, num, TINY / 2, rz2, ALU.add, ALU.mult).then_inc(s_n2, 1)
                dve.wait_ge(s_e, g + 1)
                v.tensor_tensor(ez, ez, zv, ALU.mult).then_inc(s_n3, 1)
                dve.wait_ge(s_n2, g + 1)
                dve.wait_ge(s_n3, g + 1)
                v.scalar_tensor_tensor(num, ez, 1.0 / math.sqrt(2 * math.pi), num, ALU.mult, ALU.add).then_inc(s_gp, 1)
                dve.wait_ge(s_gp, g + 1)
                dve.wait_ge(s_da, g + 1)
                wait(dve, s_g0, g)
                v.tensor_tensor(dz, num, pa[:], ALU.mult).then_inc(s_dz, 1)

            def memory(i, first, last):
                slot(2 * i, 0, True)
                slot(2 * i + 1, 1, not last)
            in_pairs(dve, memory)

            dve.wait_ge(s_g0, NG)
            dve.wait_ge(s_g1, NG)
            v.tensor_copy(g0raw[:], pg[:, 0:H]).then_inc(s_ups, 1)
            v.tensor_copy(g1T[:], pg[:, H:2 * H]).then_inc(s_ups, 1)
            dve.wait_ge(s_up, 1)
            v.scalar_tensor_tensor(fw0[:], w0_s[:], 1.0 - ALPHA, ph[:, 0:H], ALU.mult, ALU.add).then_inc(s_ups, 1)
            dve.wait_ge(s_up, 2)
            v.scalar_tensor_tensor(fw1[:], w1_s[:], 1.0 - ALPHA, pe_[0][:, 0:H].rearrange("p (c d) -> p c d", c=2),
                                   ALU.mult, ALU.add).then_inc(s_ups, 1)
            dve.wait_ge(s_up, 3)
            v.tensor_copy(wqz[:], pe_[1][:, 0:H]).then_inc(s_ups, 1)

            def logits_copy(g):
                dve.wait_ge(s_lg, g + 1)
                v.tensor_tensor(logits[:, bass.ds(g * GT, GT), :], pe_[1][:, 0:GT * E].rearrange("p (t e) -> p t e", t=GT),
                                br_bc[:].unsqueeze(1).to_broadcast([P, GT, E]), ALU.add).then_inc(s_lgs, 1)

            def recall(i, first, last):
                for par in range(2):
                    g = 2 * i + par
                    dve.wait_ge(s_h1, g + 1)
                    here = rows[:, bass.ds(g * GT, GT), 0:D]
                    v.tensor_tensor(here, ph[:].rearrange("p (t d) -> p t d", t=GT), here, ALU.add).then_inc(s_h1s, 1)
                    bn(g, s_h1s, s_bn2, s_ag2)
                    newton(rstd, g, s_nw2)
                    v.scalar_tensor_tensor(nmr[:], mv[:, :, 0], -1.0, rstd[:], ALU.mult, ALU.mult).then_inc(s_ag2n, 1)
                    v.tensor_copy(rows[:, bass.ds(g * GT, GT), RSTD:RSTD + 1], rstd[:].unsqueeze(2))
                    dve.wait_ge(s_ag2n, g + 1)
                    v.tensor_copy(rows[:, bass.ds(g * GT, GT), NMR:NMR + 1], nmr[:].unsqueeze(2))
                    wait(dve, s_x2T, g)
                    for t in range(GT):
                        ins = v.tensor_scalar(x2t[:, t, :], rowsf[:, bass.ds((g * GT + t) * ROW, D)],
                                              rstd[:, t:t + 1], nmr[:, t:t + 1], ALU.mult, ALU.add)
                    ins.then_inc(s_xn2, 1)
                    if not (first and par == 0):
                        logits_copy(g - 1)
            in_pairs(dve, recall)
            logits_copy(NG - 1)

            def b3(a):
                return a.unsqueeze(2).to_broadcast([P, NT, E])

            def red(dst, src, op):
                return v.tensor_reduce(dst, src, AX, op)

            rt = lambda ins: link(ins, s_rt)
            dve.wait_ge(s_lgs, NG)
            dve.wait_ge(s_pool0, 5)
            rt(red(m1, logits[:], ALU.max))
            lg = logits[:]
            for m, t, oh, nxt in ((m1, t0, oh0, lg2), (m2, t1, oh1, None)):
                rt(v.tensor_tensor(eqm, lg, b3(m), ALU.is_equal))
                rt(v.scalar_tensor_tensor(cand, eqm, -float(E), iota_e, ALU.mult, ALU.add))
                rt(red(t, cand, ALU.min))
                rt(v.tensor_tensor(oh, cand, b3(t), ALU.is_equal))
                if nxt is not None:
                    rt(v.scalar_tensor_tensor(nxt, oh, -BIG, lg, ALU.mult, ALU.add))
                    rt(red(m2, nxt, ALU.max))
                    lg = nxt
            link(v.tensor_tensor(den, m2, m1, ALU.subtract), s_top)
            dve.wait_ge(s_rtact, 1)
            rt(v.tensor_scalar(den, ex, 1.0, None, ALU.add))
            rt(v.reciprocal(s0, den))
            rt(v.tensor_tensor(s1, ex, s0, ALU.mult))
            dve.wait_ge(s_cnt, 1)
            rt(v.tensor_reduce(full0, pz[:, 0:fE].rearrange("p (j e) -> p e j", e=E), AX, ALU.add))
            rt(v.tensor_reduce(full1, pz[:, 512:512 + fE].rearrange("p (j e) -> p e j", e=E), AX, ALU.add))
            for full, oh, k in ((full0, oh0, k0), (full1, oh1, k1)):
                rt(v.tensor_scalar(full, full, float(TOK), None, ALU.is_ge))
                rt(v.tensor_tensor(kk, full, oh[:, NT - 1, :], ALU.mult))
                rt(v.tensor_reduce(k, kk, AX, ALU.add))
                rt(v.tensor_tensor(k, k, lastp[:], ALU.mult))
            rt(v.tensor_scalar(imax, t0, float(E), None, ALU.add))
            rt(v.tensor_scalar(pos, t1, float(E), None, ALU.add))
            L = slice(NT - 1, NT)
            for idx, k in ((imax, k0), (pos, k1)):
                rt(v.tensor_scalar(kk[:, 0:1], k, -1.0, 1.0, ALU.mult, ALU.add))
                rt(v.tensor_tensor(idx[:, L], idx[:, L], kk[:, 0:1], ALU.mult))
            rt(v.tensor_tensor(imax, imax, pos, ALU.max))
            link(v.tensor_tensor(ohm, iota_e, b3(imax), ALU.is_equal), s_ohm)
            rt(v.tensor_tensor(kk[:, 0:1], s0[:, L], k0, ALU.mult))
            rt(v.tensor_tensor(kk[:, 1:2], s1[:, L], k1, ALU.mult))
            rt(v.tensor_tensor(cx, kk[:, 0:1], kk[:, 1:2], ALU.add))
            rt(v.tensor_tensor(pos, s0, s1, ALU.add))
            rt(v.tensor_tensor(s0[:, L], s0[:, L], kk[:, 0:1], ALU.subtract))
            rt(v.tensor_tensor(s1[:, L], s1[:, L], kk[:, 1:2], ALU.subtract))
            rt(v.tensor_tensor(pos[:, L], s0[:, L], s1[:, L], ALU.add))
            rt(v.tensor_copy(rows[:, :, SCORE], pos))
            lr = rows[:, NT - 1, :]
            rt(v.scalar_tensor_tensor(lr[:, 0:D], x2t[:, GT - 1, :], cx, lr[:, 0:D], ALU.mult, ALU.add))
            rt(v.tensor_scalar(kk[:, 0:1], lr[:, RSTD:RSTD + 1], cx, 1.0, ALU.mult, ALU.add))
            rt(v.reciprocal(kk[:, 1:2], kk[:, 0:1]))
            link(v.tensor_scalar(lr[:, RSTD:NMR + 1], lr[:, RSTD:NMR + 1], kk[:, 1:2], None, ALU.mult), s_rows)
            rt(v.memset(ones_f, 1.0))
            dve.wait_ge(s_rank, 1)
            tot = pa[:, 512:512 + fE].rearrange("p (j e) -> p j e", e=E)
            for e in range(E):
                ins = v.tensor_tensor_scan(incl[:, :, e], ones_f, tot[:, :, e], 0.0, ALU.mult, ALU.add)
            rt(ins)
            rt(v.tensor_scalar(nt_i, incl[:, NT - 1, :], float(P - 1), None, ALU.add))
            rt(v.tensor_scalar(nt_i, nt_i, 7, None, ALU.arith_shift_right))
            rt(v.tensor_copy(nt_f, nt_i))
            rt(v.tensor_tensor_scan(nt_c, ones_f[:, 0:E], nt_f, 0.0, ALU.mult, ALU.add))
            rt(v.tensor_tensor(first, nt_c, nt_f, ALU.subtract))
            rt(v.tensor_scalar(nt_f, first, float(P), None, ALU.mult))
            rt(v.tensor_tensor(base, incl, tot, ALU.subtract))
            rt(v.tensor_tensor(base, base, pa[:, 0:fE].rearrange("p (j e) -> p j e", e=E), ALU.add))
            rt(v.tensor_tensor(base, base, nt_f.unsqueeze(1).to_broadcast([P, NT, E]), ALU.add))
            rt(v.tensor_tensor(base, base, ohm, ALU.mult))
            rt(red(pos, base, ALU.add))
            rt(v.tensor_copy(pos_i, pos))
            rt(v.tensor_scalar(a_i, pos_i, 7, None, ALU.arith_shift_right))
            rt(v.tensor_scalar(b_i, pos_i, P - 1, None, ALU.bitwise_and))
            rt(v.tensor_copy(slot_a, a_i))
            rt(v.tensor_copy(slot_b, b_i))
            wb = colf[:].unsqueeze(1)
            halves = 2
            nh = NT // halves
            for q in range(halves):
                J = slice(q * nh, (q + 1) * nh)
                rt(v.tensor_tensor(oh_a[:, J, :], wb[:, :, 0:NSP].to_broadcast([P, nh, NSP]),
                                   slot_a[:, J].unsqueeze(2).to_broadcast([P, nh, NSP]), ALU.is_equal))
                rt(v.tensor_tensor(val_a[:, J, 0, :], oh_a[:, J, :], tilef[:, J].unsqueeze(2).to_broadcast([P, nh, NSP]), ALU.mult))
                rt(v.tensor_scalar(val_a[:, J, 1, :], oh_a[:, J, :], rowp1[:], None, ALU.mult))
                ins = v.tensor_tensor(oh_b[:, J, :], wb.to_broadcast([P, nh, P]),
                                      slot_b[:, J].unsqueeze(2).to_broadcast([P, nh, P]), ALU.is_equal)
                ins.then_inc(s_onehot, 1)
            rt(v.tensor_tensor(starts, starts, first.unsqueeze(1).to_broadcast([P, NS, E]), ALU.is_ge))
            rt(v.tensor_reduce(tile_e, starts, AX, ALU.add))
            rt(v.tensor_scalar(exp_idx[:, 0:NS], tile_e, -1.0, None, ALU.add))
            dve.wait_ge(s_slots, 1)
            rt(v.tensor_copy(slot_v[:], pe_[0][:, NSP:2 * NSP]))
            rt(v.scalar_tensor_tensor(slot_v[:], pe_[0][:, 0:NSP], float(P), slot_v[:], ALU.mult, ALU.add))
            rt(v.tensor_scalar(slot_idx[:, :, 0], slot_v[:], -1.0, 0.0, ALU.add, ALU.max))
            rt(v.tensor_scalar(val0[:], slot_v[:], 0.0, SKIP, ALU.is_equal, ALU.mult))
            link(v.scalar_tensor_tensor(slot_idx[:, :, 1], slot_v[:], -1.0, val0[:], ALU.add, ALU.add), s_table)

            def in_copy(a, k):
                dve.wait_ge(s_xgT, a + 1)
                wait(dve, s_u, 2 * a - 2)
                v.tensor_copy(xgF[k % 2], ph[:, 0:P]).then_inc(s_xgF, 1)

            def gelu_copy(a, k):
                dve.wait_ge(s_eaT, a + 1)
                wait(dve, s_y, a - 1)
                v.tensor_copy(act_eF[k % 2], pe_[0][:]).then_inc(s_eaF, 1)

            def out_rows(a, k, i):
                dve.wait_ge(s_y, a + 1)
                if isinstance(a, int):
                    wait(dve, s_put[k % 2], 16 * ((a - 2) // 2 + 1))
                else:
                    dve.wait_ge(s_put[k % 2], 16 * (i * (RING // 2) + (k - 2) // 2 + 1))
                r = got[k % RING]
                v.scalar_tensor_tensor(outs[k % 2], pe_[1][:, 0:D], r[:, SCORE:SCORE + 1], r[:, 0:D],
                                       ALU.mult, ALU.add).then_inc(s_o, 1)

            in_copy(0, 0)

            def experts(i, first_, last_):
                for k in range(RING):
                    a = RING * i + k
                    if not (last_ and a >= NS):
                        dve.wait_ge(s_u, 2 * a + 2)
                        dve.wait_ge(s_u1, a + 1)
                        wait(dve, s_ea, a - 1)
                        v.tensor_tensor(hid[k % 2], u1s[k % 2], (pz, pa)[k % 2][:, F:2 * F], ALU.mult).then_inc(s_hid, 1)
                        if not (last_ and a + 1 >= NS):
                            in_copy(a + 1, k + 1)
                    if not (first_ and k < 2) and not (last_ and a - 2 >= NS):
                        out_rows(a - 2, k - 2, i)
                    if not (first_ and k < 1) and not (last_ and a - 1 >= NS):
                        gelu_copy(a - 1, k - 1)
            in_rings(dve, experts)
            n = (NS + RING - 1) // RING
            for a in range(n * RING - 2, NS):
                out_rows(a, a % RING, 0)

        @block.tensor
        def _(pe):
            mm, tr = nc.tensor.matmul, nc.tensor.transpose
            pe.wait_ge(s_const, 1)
            pe.wait_ge(s_w, 16 * 9)
            for n in range(NGRAM):
                tr(pz[:, n * D:(n + 1) * D], proj_s[:, n * D:(n + 1) * D], ident[:])
            tr(pa[:, 0:D], wk_s[:], ident[:])
            tr(pa[:, D:2 * D], wq_s[:], ident[:])
            tr(pa[:, 2 * D:3 * D], w1_s[:, 0, :], ident[:])
            tr(pa[:, 3 * D:4 * D], w1_s[:, 1, :], ident[:]).then_inc(s_wT, 1)
            pe.wait_ge(s_hash, 1)
            tr(pg[:, 0:NT], h2[:, 2:2 + P], ident[0:NT, 0:NT])
            tr(pg[:, NT:2 * NT], h3[:, 3:3 + P], ident[0:NT, 0:NT])
            tr(pg[:, 2 * NT:3 * NT], h4[:, 3:3 + P], ident[0:NT, 0:NT]).then_inc(s_hT, 1)
            pe.wait_ge(s_wTs, 5)
            mm(ph[:, 0:H], wkT[:], w0_s[:], start=True, stop=True).then_inc(s_wkz, 1)
            pe.wait_ge(s_idx, 1)
            pe.wait_ge(s_wkzs, 1)

            def emb_T(g, par, i):
                for n in range(NGRAM):
                    pe.wait_ge(s_gath[par][n], 16 * GT * (i + 1))
                    wait(pe, s_eF[(n + 1) % NGRAM], g if n < 2 else g + 1)
                    for t in range(GT):
                        ins = tr(pe_[(NGRAM * par + n) % 2][:, t * P:(t + 1) * P], gath[par][:, n, t, :], ident[:])
                    ins.then_inc(s_eT[n], 1)

            def h0_mm(g, par):
                for n in range(NGRAM):
                    pe.wait_ge(s_eF[n], g + 1)
                wait(pe, s_xF, g)
                for t in range(GT):
                    for n in range(NGRAM):
                        ins = mm(ph[:, t * P:(t + 1) * P], embF[par][:, n, t * P:(t + 1) * P], projT[:, n, :],
                                 start=(n == 0), stop=(n == NGRAM - 1))
                ins.then_inc(s_h0, 1)

            def xn_T(g, par):
                pe.wait_ge(s_xn, g + 1)
                for t in range(GT):
                    ins = tr(ph[:, t * P:(t + 1) * P], xnT[par][:, t, :], ident[:])
                ins.then_inc(s_xT, 1)

            def grad0(g, par, start):
                pe.wait_ge(s_dz, g + 1)
                for t in range(GT):
                    ins = mm(pg[:, 0:H], xnT[par][:, t, :], dz[:, t * H:(t + 1) * H],
                             start=False, stop=False, skip_group_check=True)
                ins.then_inc(s_g0, 1)

            emb_T(0, 0, 0)
            h0_mm(0, 0)
            xn_T(0, 0)

            def slot(g, par, i, is_first, has_next):
                pe.wait_ge(s_xF, g + 1)
                wait(pe, s_n3, g)
                for t in range(GT):
                    ins = mm(pz[:, t * H:(t + 1) * H], xnF[par][:, t * P:(t + 1) * P], wkz[:], start=True, stop=True)
                ins.then_inc(s_z, 1)
                if not is_first:
                    grad0(g - 1, 1 - par, False)
                if has_next:
                    emb_T(g + 1, 1 - par, i if par == 0 else i + 1)
                pe.wait_ge(s_act, g + 1)
                for t in range(GT):
                    for c in range(2):
                        ins = tr(pa[:, c * GTOK + t * P:c * GTOK + (t + 1) * P], act_t[:, t * H + c * P:t * H + (c + 1) * P], ident[:])
                ins.then_inc(s_aT, 1)
                if has_next:
                    h0_mm(g + 1, 1 - par)
                pe.wait_ge(s_aF, g + 1)
                for t in range(GT):
                    T = slice(t * P, (t + 1) * P)
                    mm(pa[:, T], act_f[:, T], w1_s[:, 0, :], start=True, stop=False)
                    mm(pa[:, T], act_f[:, GTOK + t * P:GTOK + (t + 1) * P], w1_s[:, 1, :], start=False, stop=False)
                    ins = mm(pa[:, T], xnF[par][:, T], nwv[:], start=False, stop=True)
                ins.then_inc(s_m, 1)
                pe.wait_ge(s_res, g + 1)
                for t in range(GT):
                    ins = tr(pa[:, GTOK + t * P:GTOK + (t + 1) * P], res_t[:, t * P:(t + 1) * P], ident[:])
                ins.then_inc(s_rT, 1)
                for t in range(GT):
                    one = is_first and t == 0
                    ins = mm(pg[:, H:2 * H], res_t[:, t * P:(t + 1) * P], act_t[:, t * H:(t + 1) * H],
                             start=one, stop=False, skip_group_check=True)
                ins.then_inc(s_g1, 1)
                if has_next:
                    xn_T(g + 1, 1 - par)
                pe.wait_ge(s_rF, g + 1)
                for t in range(GT):
                    ins = mm(pa[:, t * H:(t + 1) * H], res_f[:, t * P:(t + 1) * P], w1T[:], start=True, stop=True)
                ins.then_inc(s_da, 1)

            def memory(i, first, last):
                slot(2 * i, 0, i, first, True)
                slot(2 * i + 1, 1, i, False, not last)
            in_pairs(pe, memory)
            grad0(NG - 1, 1, False)

            pe.wait_ge(s_ups, 2)
            mm(ph[:, 0:H], wk_s[:], g0raw[:], start=True, stop=True).then_inc(s_up, 1)
            tr(pe_[0][:, 0:D], g1T[:, 0:D], ident[:])
            tr(pe_[0][:, D:H], g1T[:, D:H], ident[:]).then_inc(s_up, 1)
            pe.wait_ge(s_ups, 3)
            mm(pe_[1][:, 0:H], wqT[:], fw0[:], start=True, stop=True).then_inc(s_up, 1)
            pe.wait_ge(s_ups, 5)
            for par in range(2):
                pe.wait_ge(s_xall[par], 16 * (NG // 2))

            pq = [pz, pa]

            def query(g, par):
                wait(pe, s_a2, g - 1)
                for c in range(2):
                    ins = mm(pq[par][:, c * GTOK:(c + 1) * GTOK], wqz[:, c * P:(c + 1) * P],
                             xnF_all[:, bass.ds(g * GTOK, GTOK)], start=True, stop=True)
                ins.then_inc(s_q, 1)

            def x2_T(g):
                pe.wait_ge(s_xn2, g + 1)
                wait(pe, s_x2F, g)
                for t in range(GT):
                    ins = tr(pe_[0][:, t * P:(t + 1) * P], x2t[:, t, :], ident[:])
                ins.then_inc(s_x2T, 1)

            def logit_mm(g):
                pe.wait_ge(s_x2F, g + 1)
                wait(pe, s_lgs, g)
                for t in range(GT):
                    ins = mm(pe_[1][:, t * E:(t + 1) * E], x2f[:, t * P:(t + 1) * P], wr_s[:], start=True, stop=True)
                ins.then_inc(s_lg, 1)

            query(0, 0)

            def recall(i, first, last):
                for par in range(2):
                    g = 2 * i + par
                    if not (last and par == 1):
                        query(g + 1, 1 - par)
                    if not (first and par == 0):
                        x2_T(g - 1)
                    pe.wait_ge(s_a2, g + 1)
                    wait(pe, s_h1s, g)
                    for t in range(GT):
                        for c in range(2):
                            ins = mm(ph[:, t * P:(t + 1) * P], act2[par][:, c * GTOK + t * P:c * GTOK + (t + 1) * P],
                                     fw1[:, c, :], start=(c == 0), stop=(c == 1))
                    ins.then_inc(s_h1, 1)
                    if not (first and par == 0):
                        logit_mm(g - 1)
            in_pairs(pe, recall)
            x2_T(NG - 1)
            logit_mm(NG - 1)

            pe.wait_ge(s_top, 1)
            mm(pz[:, 0:fE], ones_bf[:], oh0, start=True, stop=True)
            mm(pz[:, 512:512 + fE], ones_bf[:], oh0, start=True, stop=False)
            mm(pz[:, 512:512 + fE], ones_bf[:], oh1, start=False, stop=True).then_inc(s_cnt, 1)
            pe.wait_ge(s_ohm, 1)
            mm(pa[:, 0:fE], before[:], ohm, start=True, stop=True)
            mm(pa[:, 512:512 + fE], ones_bf[:], ohm, start=True, stop=True).then_inc(s_rank, 1)
            for j in range(NT):
                if j % (NT // 2) == 0:
                    pe.wait_ge(s_onehot, j // (NT // 2) + 1)
                ins = mm(pe_[0][:, 0:2 * NSP], oh_b[:, j, :], val_a[:, j, :, :].rearrange("p v a -> p (v a)"),
                         start=(j == 0), stop=(j == NT - 1))
            ins.then_inc(s_slots, 1)

            pe.wait_ge(s_f, 48)
            pe.wait_ge(s_table, 1)

            def in_T(a, k):
                pe.wait_ge(s_xg, a + 1)
                wait(pe, s_xgF, a)
                tr(ph[:, 0:P], xg[k % 2], ident[:]).then_inc(s_xgT, 1)

            def down(a, k):
                e = pe.value_load(exp_idx[0:1, bass.ds(a, 1)], min_val=0, max_val=E - 1)
                pe.wait_ge(s_eaF, a + 1)
                wait(pe, s_o, a)
                for c in range(4):
                    ins = mm(pe_[1][:, 0:D], act_eF[k % 2][:, c * P:(c + 1) * P], f3_f[:, bass.ds(e * F + c * D, D)],
                             start=(c == 0), stop=(c == 3))
                ins.then_inc(s_y, 1)

            def gelu_T(a, k):
                pe.wait_ge(s_ea, a + 1)
                wait(pe, s_eaF, a)
                for c in range(4):
                    ins = tr(pe_[0][:, c * P:(c + 1) * P], act_e[k % 2][:, c * P:(c + 1) * P], ident[:])
                ins.then_inc(s_eaT, 1)

            in_T(0, 0)

            def experts(i, first, last):
                for k in range(RING):
                    a = RING * i + k
                    if not (last and a >= NS):
                        e = pe.value_load(exp_idx[0:1, bass.ds(a, 1)], min_val=0, max_val=E - 1)
                        pu = (pz, pa)[k % 2]
                        pe.wait_ge(s_xgF, a + 1)
                        wait(pe, s_hid, a - 1)
                        mm(pu[:, 0:F], xgF[k % 2], f2_f[:, bass.ds(e * F, F)], start=True, stop=True).then_inc(s_u, 1)
                        mm(pu[:, F:2 * F], xgF[k % 2], f1_f[:, bass.ds(e * F, F)], start=True, stop=True).then_inc(s_u, 1)
                        if not (last and a + 1 >= NS):
                            in_T(a + 1, k + 1)
                    if not (first and k < 2) and not (last and a - 2 >= NS):
                        down(a - 2, k - 2)
                    if not (first and k < 1) and not (last and a - 1 >= NS):
                        gelu_T(a - 1, k - 1)
            in_rings(pe, experts)
            n = (NS + RING - 1) // RING
            for a in range(n * RING - 2, NS):
                down(a, a)


_INS = ['x', 'L0_tok_emb_2', 'L0_tok_emb_3', 'L0_tok_emb_4', 'L0_tok_proj_w', 'L0_tok_proj_b', 'L0_attn_w_k',
        'L0_attn_w_v', 'L0_attn_w_q', 'L0_attn_W0', 'L0_attn_W1', 'L0_ffn_Wr', 'L0_ffn_br', 'L0_ffn_W1',
        'L0_ffn_W2', 'L0_ffn_W3']
_OUTS = [((BATCH, SEQ, D), 'float32')]


def kernel(**inputs):
    import numpy as _np
    import concourse.bacc as _bacc
    from concourse import mybir as _mybir
    from concourse.bass_utils import run_bass_kernel_spmd as _run

    nc = _bacc.Bacc("TRN2", target_bir_lowering=False, num_devices=1)
    arrays, args = {}, []
    for name in _INS:
        a = _np.ascontiguousarray(inputs[name])
        arrays[f"in_{name}_dram"] = a
        args.append(nc.dram_tensor(f"in_{name}_dram", a.shape, _mybir.dt.from_np(a.dtype), kind="ExternalInput").ap())
    for i, (shape, dtype) in enumerate(_OUTS):
        dt = _mybir.dt.from_np(_np.dtype(dtype))
        args.append(nc.dram_tensor(f"out_{i}_dram", shape, dt, kind="ExternalOutput").ap())
    tower(nc, *args)
    r = _run(nc, [arrays], core_ids=[0])
    return r.results[0]["out_0_dram"]
```

```python
import math
from contextlib import ExitStack

import concourse.bass as bass
from concourse import mybir

P = 128
BATCH, SEQ = 8, 1024
TOK = BATCH * SEQ
D = 128
H = 256
F = 512
E = 8
NGRAM = 3
VOCAB = 25000
CHUNK = 64
NCHUNK = SEQ // CHUNK
NT = TOK // P
GT = 4
GTOK = GT * P
NG = TOK // GTOK
GPS = SEQ // GTOK
NS = NT + E - 1
ROW = 132
RSTD, NMR, SCORE = 128, 129, 130
RING = 8
LAG = 6
ALPHA, LR, DECAY = 0.1, 0.01, 0.9
EPS = 1e-5
TINY = 2.0 ** -60
GRAD = -LR * 2.0 / (BATCH * CHUNK * D)
MAGIC = float(0x5F3759DF)
SKIP = float(1 << 20)
BIG = 3.0e38


def wait(eng, sem, value):
    if isinstance(value, int) and value <= 0:
        return
    eng.wait_ge(sem, value)


def tower(nc, x, emb2, emb3, emb4, proj_w, proj_b, w_k, w_v, w_q, W0, W1, Wr, br, F1, F2, F3, out):
    f32, bf16, i32 = mybir.dt.float32, mybir.dt.bfloat16, mybir.dt.int32
    ALU, ACT, AX = mybir.AluOpType, mybir.ActivationFunctionType, mybir.AxisListType.X
    tables = [emb2, emb3, emb4]
    ctx = ExitStack()
    with ctx:
        def sb(name, shape, dt=f32):
            return ctx.enter_context(nc.sbuf_tensor(name, shape, dt))

        def sem(name):
            return ctx.enter_context(nc.semaphore(name))

        colf = sb("colf", [P, P])
        rowf = sb("rowf", [P, 1])
        ident = sb("ident", [P, P])
        before = sb("before", [P, P], bf16)
        ones_bf = sb("ones_bf", [P, P], bf16)
        tilef = sb("tilef", [P, NT])
        decay = sb("decay", [P, GPS, GT])
        lastp = sb("lastp", [P, 1])
        tiny_c = sb("tiny_c", [P, 1])
        rowp1 = sb("rowp1", [P, 1])
        proj_s = sb("proj_s", [P, NGRAM * D])
        projT = sb("projT", [P, NGRAM, D])
        bias_bc = sb("bias_bc", [P, D])
        br_bc = sb("br_bc", [P, E])
        wk_s, wv_s, wq_s = sb("wk_s", [P, D]), sb("wv_s", [P, D]), sb("wq_s", [P, D])
        wkT, wqT, nwv = sb("wkT", [P, D]), sb("wqT", [P, D]), sb("nwv", [P, D])
        w0_s = sb("w0_s", [P, H])
        w1_s = sb("w1_s", [P, 2, D])
        w1T = sb("w1T", [P, H])
        wkz = sb("wkz", [P, H])
        g0raw = sb("g0raw", [P, H])
        g1T = sb("g1T", [P, H])
        fw0 = sb("fw0", [P, H])
        fw1 = sb("fw1", [P, 2, D])
        wqz = sb("wqz", [P, H])
        wr_s = sb("wr_s", [P, E])
        f1_s = sb("f1_s", [P, E, F])
        f2_s = sb("f2_s", [P, E, F])
        f3_s = sb("f3_s", [P, E, 4, D])
        f1_f, f2_f = (t[:].rearrange("p e f -> p (e f)") for t in (f1_s, f2_s))
        f3_f = f3_s[:].rearrange("p e c d -> p (e c d)")
        rows = sb("rows", [P, NT, ROW])
        xnF_all = sb("xnF_all", [P, TOK])
        rowsf = rows[:].rearrange("p j c -> p (j c)")
        logits = sb("logits", [P, NT, E])
        work = sb("work", [P, 16384])
        at = [0]

        def carve(cols, dt=f32):
            a = at[0]
            at[0] += cols
            assert at[0] <= 16384, at[0]
            v = work[:, a:a + cols]
            return v if dt is f32 else v.bitcast(dt)

        gath = [carve(NGRAM * GTOK).rearrange("p (n t d) -> p n t d", n=NGRAM, t=GT) for _ in range(2)]
        embF = [carve(NGRAM * GTOK).rearrange("p (n c) -> p n c", n=NGRAM) for _ in range(2)]
        xnT = [carve(GTOK).rearrange("p (t d) -> p t d", t=GT) for _ in range(2)]
        xnF = [carve(GTOK) for _ in range(2)]
        act_t = carve(GT * H)
        act_f = carve(2 * GTOK)
        zsq, rz2, ez = (carve(GT * H) for _ in range(3))
        lnz = rz2
        num = carve(GT * H)
        dz = carve(GT * H)
        res_t = carve(GTOK)
        res_f = sb("res_f", [P, GTOK])
        idx_all = sb("idx_all", [P, NGRAM, NT], i32)
        idx_g = [sb(f"idx_g{k}", [P, NGRAM, GT], i32) for k in range(2)]
        stats, mv = sb("stats", [P, GT, 6]), sb("mv", [P, 2 * GT, 2])
        ve, seed, ya, yb, rstd = (sb(n, [P, 2 * GT]) for n in ("ve", "seed", "ya", "yb", "rstd"))
        nmr = sb("nmr", [P, 2 * GT])
        at[0] = 0
        act2 = [carve(2 * GTOK) for _ in range(2)]
        x2t = [carve(GTOK).rearrange("p (t d) -> p t d", t=GT) for _ in range(2)]
        x2f = carve(GTOK)
        fE = NT * E
        big3 = lambda v: v.rearrange("p (j e) -> p j e", e=E)
        iota_e = big3(carve(fE))
        eqm, cand, lg2 = big3(carve(fE)), big3(carve(fE)), big3(carve(fE))
        oh0, oh1, ohm = (big3(carve(fE // 2, bf16)) for _ in range(3))
        incl, base = big3(carve(fE)), big3(carve(fE))
        m1, m2, t0, t1, imax, ex, den, s0, s1, pos = (carve(NT) for _ in range(10))
        slot_a, slot_b = carve(NT), carve(NT)
        pos_i, a_i, b_i = (carve(NT, i32) for _ in range(3))
        ones_f = carve(NT)
        full0, full1, k0, k1, kk, cx = carve(E), carve(E), carve(1), carve(1), carve(E), carve(1)
        nt_f, nt_i, nt_c, first = carve(E), carve(E, i32), carve(E), carve(E)
        starts = carve(NS * E).rearrange("p (a e) -> p a e", e=E)
        tile_e = carve(NS)
        oh_b = xnF_all[:, 0:NT * P // 2].bitcast(bf16).rearrange("p (j b) -> p j b", b=P)
        NSP = NS + 1
        oh_a = xnF_all[:, 4096:4096 + NT * NSP // 2].bitcast(bf16).rearrange("p (j a) -> p j a", a=NSP)
        val_a = work[:, 9216:9216 + NT * NSP].bitcast(bf16).rearrange("p (j v a) -> p j v a", v=2, a=NSP)
        assert at[0] <= 9216, at[0]
        slot_v = sb("slot_v", [P, NSP])
        val0 = sb("val0", [P, NSP])
        slot_idx = sb("slot_idx", [P, NSP, 2], i32)
        slot_if = slot_idx[:].rearrange("p a v -> p (a v)")
        exp_idx = sb("exp_idx", [P, NSP], i32)
        at[0] = 0
        got = [sb(f"got{k}", [P, ROW]) for k in range(RING)]
        idx_s = [sb(f"idx_s{k}", [P, 2], i32) for k in range(RING)]
        xg = [carve(P) for _ in range(2)]
        xgF = [carve(P) for _ in range(2)]
        u1s = [carve(F) for _ in range(2)]
        hid = [carve(F) for _ in range(2)]
        act_e = [carve(F) for _ in range(2)]
        act_eF = [carve(F) for _ in range(2)]
        outs = [carve(P) for _ in range(2)]
        HW = P + 3
        at[0] = 0
        xw = carve(HW, i32)[0:NT]
        hb, h2, h3, h4, vv, rr, tt = (carve(HW)[0:NT] for _ in range(7))
        qi = carve(HW, i32)[0:NT]
        pz = ctx.enter_context(nc.psum_tensor("pz", [P, 1024], f32))
        pa = ctx.enter_context(nc.psum_tensor("pa", [P, 1024], f32))
        pe_ = [ctx.enter_context(nc.psum_tensor(f"pe{k}", [P, 512], f32)) for k in range(2)]
        ph = ctx.enter_context(nc.psum_tensor("ph", [P, 512], f32))
        pg = ctx.enter_context(nc.psum_tensor("pg", [P, 512], f32))
        rows_d = nc.dram_tensor("rows_d", (TOK, ROW), f32).ap()

        s_x, s_w, s_f, s_row = sem("x_loaded"), sem("weights_loaded"), sem("experts_loaded"), sem("rows_stored")
        s_const, s_pool0, s_hz = sem("constants_made"), sem("iotas_made"), sem("x_zeroed")
        s_hstep, s_hash = sem("hash_step"), sem("hashes_made")
        s_hT, s_idx = sem("hashes_transposed"), sem("indices_made")
        s_wT, s_wTs, s_wkz, s_wkzs = sem("weights_transposed"), sem("weight_copies"), sem("wkz_in_psum"), sem("wkz_made")
        s_icopy = [sem(f"group_indices{k}") for k in range(2)]
        s_gath = [[sem(f"gathered{k}_{n}") for n in range(NGRAM)] for k in range(2)]
        s_eT = [sem(f"embedding_transposed{n}") for n in range(NGRAM)]
        s_eF = [sem(f"embedding_copied{n}") for n in range(NGRAM)]
        s_h0, s_h0s = sem("h0_in_psum"), sem("h0_copied")
        s_bn, s_ag, s_nw, s_xn = sem("stats_made"), sem("stats_joined"), sem("newton_step"), sem("normed")
        s_xT, s_xF, s_xall = sem("normed_transposed"), sem("normed_copied"), [sem(f"normed_kept{k}") for k in range(2)]
        s_z, s_act, s_sq, s_ln, s_r, s_e = (sem(n) for n in ("z_in_psum", "gelu_made", "z_squared", "log_made", "inverse_made", "exp_made"))
        s_aT, s_aF = sem("gelu_transposed"), sem("gelu_copied")
        s_m, s_res, s_rT, s_rF, s_g1 = (sem(n) for n in ("residual_in_psum", "residual_made", "residual_transposed", "residual_copied", "grad1_added"))
        s_n1, s_n2, s_n3, s_gp = (sem(n) for n in ("gz_made", "phi_made", "ez_made", "slope_made"))
        s_da, s_dz, s_g0 = sem("da_in_psum"), sem("dz_made"), sem("grad0_added")
        s_gz = sem("gradients_zeroed")
        s_up, s_ups = sem("update_in_psum"), sem("update_copied")
        s_q, s_a2, s_h1, s_h1s = sem("zq_in_psum"), sem("gelu2_made"), sem("h1_in_psum"), sem("h1_copied")
        s_pair = sem("pair_scales_made")
        s_bn2, s_ag2, s_nw2, s_xn2 = sem("stats2_made"), sem("stats2_joined"), sem("newton2_step"), sem("normed2")
        s_x2T, s_x2F, s_lg, s_lgs = (sem(n) for n in ("normed2_transposed", "normed2_copied", "logits_in_psum", "logits_copied"))
        s_rt, s_top, s_rtact, s_cnt, s_rank, s_ohm, s_rows = (sem(n) for n in (
            "route_step", "top_two_found", "score_exp", "choices_counted", "ranks_in_psum", "choice_ready", "rows_ready"))
        s_onehot, s_slots, s_table = sem("one_hots_made"), sem("slots_in_psum"), sem("slot_table_made")
        s_is = sem("slot_indices_copied")
        s_got = [sem(f"rows_gathered{k}") for k in range(RING)]
        s_put = [sem(f"rows_scattered{k}") for k in range(2)]
        s_xg, s_xgT, s_xgF = sem("expert_in_normed"), sem("expert_in_transposed"), sem("expert_in_copied")
        s_u, s_u1, s_hid, s_ea, s_eaT, s_eaF = (sem(n) for n in ("up_in_psum", "up1_copied", "hidden_made", "expert_gelu", "expert_gelu_transposed", "expert_gelu_copied"))
        s_y, s_o = sem("expert_out_in_psum"), sem("expert_out_made")

        def alone(eng, sem, value):
            if not isinstance(value, int):
                value = eng.to_reg(value)
            eng.wait_ge(s_const, 1)
            eng.wait_ge(sem, value)

        NSTEP = 12
        block = ctx.enter_context(nc.Block())

        def in_pairs(eng, body, lag=0):
            for i in range(1 + lag):
                body(i, i == 0, False)
            with eng.Fori(1 + lag, NG // 2 - 1) as i:
                body(i, False, False)
            body(NG // 2 - 1, False, True)

        def in_rings(eng, body):
            n = (NS + RING - 1) // RING
            body(0, True, False)
            with eng.Fori(1, n - 1) as i:
                body(i, False, False)
            body(n - 1, False, True)

        @block.sync
        def _(sp):
            xt = x.rearrange("b (j p) -> (b j) p", p=P)
            sp.wait_ge(s_hz, 1)
            sp.dma_start(xw[:, 2:2 + P], xt).then_inc(s_x, 16)
            sp.dma_start(xw[1:NT, 0:2], xt[0:NT - 1, P - 2:P]).then_inc(s_x, 16)
            sp.dma_start(xw[0:NT - 1, 2 + P:3 + P], xt[1:NT, 0:1], allow_slow_non_contiguous=True).then_inc(s_x, 16)
            for dst, src in ((proj_s[:], proj_w), (wk_s[:], w_k), (wv_s[:], w_v), (wq_s[:], w_q), (w0_s[:], W0),
                             (w1_s[:], W1.rearrange("(c p) d -> p c d", p=P)), (wr_s[:], Wr),
                             (bias_bc[:], proj_b[None, :].to_broadcast([P, D])),
                             (br_bc[:], br[None, :].to_broadcast([P, E]))):
                sp.dma_start(dst, src).then_inc(s_w, 16)
            sp.dma_start(f1_s[:], F1.rearrange("e p f -> p e f")).then_inc(s_f, 16)
            sp.dma_start(f2_s[:], F2.rearrange("e p f -> p e f")).then_inc(s_f, 16)
            sp.dma_start(f3_s[:], F3.rearrange("e (c p) d -> p e c d", p=P)).then_inc(s_f, 16)

            def keep(i, first, last):
                for par in range(2):
                    g = 2 * i + par
                    sp.wait_ge(s_xF, g + 1)
                    sp.dma_start(xnF_all[:, bass.ds(g * GTOK, GTOK)], xnF[par]).then_inc(s_xall[par], 16)
            in_pairs(sp, keep)
            sp.wait_ge(s_rows, 1)
            sp.dma_start(rows_d.rearrange("(j p) c -> p j c", p=P), rows[:]).then_inc(s_row, 16)

        @block.gpsimd
        def _(pool):
            nc.gpsimd.memset(xw[:], 0).then_inc(s_hz, 1)
            nc.gpsimd.iota(colf[:], pattern=[[1, P]], base=0, channel_multiplier=0,
                           allow_small_or_imprecise_dtypes=True).then_inc(s_pool0, 1)
            nc.gpsimd.iota(rowf[:], pattern=[[0, 1]], base=0, channel_multiplier=1,
                           allow_small_or_imprecise_dtypes=True).then_inc(s_pool0, 1)
            nc.gpsimd.iota(tilef[:], pattern=[[1, NT]], base=0, channel_multiplier=0,
                           allow_small_or_imprecise_dtypes=True).then_inc(s_pool0, 1)
            pool.wait_ge(s_idx, 1)

            def gathers(i, first, last):
                for par in range(2):
                    g = 2 * i + par
                    for n in range(NGRAM):
                        wait(pool, s_eT[n], g - 1)
                    nc.gpsimd.tensor_copy(idx_g[par][:], idx_all[:, :, bass.ds(g * GT, GT)]).then_inc(s_icopy[par], 1)
                    alone(pool, s_icopy[par], i + 1)
                    for n in range(NGRAM):
                        for t in range(GT):
                            nc.gpsimd.indirect_dma_start(
                                out=gath[par][:, n, t, :], out_offset=None, in_=tables[n],
                                in_offset=bass.IndirectOffsetOnAxis(ap=idx_g[par][:, n, t:t + 1], axis=0),
                            ).then_inc(s_gath[par][n], 16)
            in_pairs(pool, gathers)

            pool.wait_ge(s_lgs, NG)
            nc.gpsimd.iota(iota_e, pattern=[[0, NT], [1, E]], base=0, channel_multiplier=0,
                           allow_small_or_imprecise_dtypes=True).then_inc(s_pool0, 1)
            nc.gpsimd.iota(starts, pattern=[[1, NS], [0, E]], base=0, channel_multiplier=0,
                           allow_small_or_imprecise_dtypes=True).then_inc(s_pool0, 1)
            pool.wait_ge(s_table, 1)
            pool.wait_ge(s_row, 16)

            def gather(a, k, i):
                if not (isinstance(a, int) and a < RING):
                    pool.wait_ge(s_put[k % 2], 16 * ((a - RING) // 2 + 1) if isinstance(a, int)
                                 else 16 * (i * (RING // 2) + (k - RING) // 2 + 1))
                nc.gpsimd.tensor_copy(idx_s[k][:], slot_if[:, bass.ds(2 * a, 2)]).then_inc(s_is, 1)
                alone(pool, s_is, a + 1)
                nc.gpsimd.indirect_dma_start(
                    out=got[k][:], out_offset=None, in_=rows_d,
                    in_offset=bass.IndirectOffsetOnAxis(ap=idx_s[k][:, 0:1], axis=0)).then_inc(s_got[k], 16)

            def scatter(a, k):
                alone(pool, s_o, a + 1)
                nc.gpsimd.indirect_dma_start(
                    out=out.rearrange("b s d -> (b s) d"), in_=outs[k % 2],
                    out_offset=bass.IndirectOffsetOnAxis(ap=idx_s[k][:, 1:2], axis=0), in_offset=None,
                    bounds_check=TOK - 1, oob_is_err=False).then_inc(s_put[k % 2], 16)

            def move(i, first, last):
                for k in range(RING):
                    a = RING * i + k
                    if not (last and a >= NS):
                        gather(a, k, i)
                    if not (first and k < LAG):
                        scatter(a - LAG, (k - LAG) % RING)
            in_rings(pool, move)
            n = (NS + RING - 1) // RING
            for a in range(n * RING - LAG, NS):
                scatter(a, a % RING)
            for par in range(2):
                pool.wait_ge(s_put[par], 16 * ((NS - par + 1) // 2))

        @block.scalar
        def _(act):
            act.wait_ge(s_w, 16 * 9)
            nc.scalar.mul(nwv[:], wv_s[:], -1.0).then_inc(s_wTs, 1)
            act.wait_ge(s_wT, 1)
            nc.scalar.copy(projT[:], pz[:, 0:NGRAM * D].rearrange("p (n d) -> p n d", n=NGRAM)).then_inc(s_wTs, 1)
            nc.scalar.copy(wkT[:], pa[:, 0:D]).then_inc(s_wTs, 1)
            nc.scalar.copy(wqT[:], pa[:, D:2 * D]).then_inc(s_wTs, 1)
            nc.scalar.copy(w1T[:], pa[:, 2 * D:2 * D + H]).then_inc(s_wTs, 1)
            act.wait_ge(s_wkz, 1)
            nc.scalar.copy(wkz[:], ph[:, 0:H]).then_inc(s_wkzs, 1)

            def emb_copy(g, par, n):
                lo = (0 if par else 1 if n < 2 else 2)
                hi = GTOK - (1 if par and n > 0 else 0)
                act.wait_ge(s_eT[n], g + 1)
                wait(act, s_h0, g - 1)
                nc.scalar.copy(embF[par][:, n, lo:hi], pe_[(NGRAM * par + n) % 2][:, lo:hi]).then_inc(s_eF[n], 1)

            def normed_copy(g, par, i):
                act.wait_ge(s_xT, g + 1)
                wait(act, s_m, 2 * (g - 1))
                wait(act, s_xall[par], 16 * i)
                nc.scalar.copy(xnF[par], ph[:]).then_inc(s_xF, 1)

            act.wait_ge(s_const, 1)
            emb_copy(0, 0, 0)
            emb_copy(0, 0, 2)
            normed_copy(0, 0, 0)

            def slot(g, par, i, is_first, has1, has2):
                act.wait_ge(s_z, g + 1)
                wait(act, s_aT, g)
                wait(act, s_g1, g)
                nc.scalar.activation(act_t, pz[:], ACT.Gelu).then_inc(s_act, 1)
                if is_first:
                    emb_copy(1, 1, 0)
                    emb_copy(1, 1, 2)
                act.wait_ge(s_aT, g + 1)
                wait(act, s_m, 2 * g)
                nc.scalar.copy(act_f, pa[:]).then_inc(s_aF, 1)
                if has2:
                    emb_copy(g + 2, par, 0)
                act.wait_ge(s_n1, g + 1)
                nc.scalar.activation(zsq, pz[:], ACT.Square).then_inc(s_sq, 1)
                act.wait_ge(s_sq, g + 1)
                wait(act, s_gp, g)
                nc.scalar.activation(lnz, zsq, ACT.Ln, bias=tiny_c[:]).then_inc(s_ln, 1)
                if has2:
                    emb_copy(g + 2, par, 2)
                act.wait_ge(s_ln, g + 1)
                nc.scalar.activation(rz2, lnz, ACT.Exp, scale=-1.0).then_inc(s_r, 1)
                if has1:
                    normed_copy(g + 1, 1 - par, i if par == 0 else i + 1)
                nc.scalar.activation(ez, zsq, ACT.Exp, scale=-0.5).then_inc(s_e, 1)

            def memory(i, first, last):
                slot(2 * i, 0, i, first, True, not last)
                slot(2 * i + 1, 1, i, False, not last, not last)
            in_pairs(act, memory)

            pq = [pz, pa]

            def queries_gelu(g, par):
                act.wait_ge(s_q, g + 1)
                wait(act, s_h1, g - 1)
                nc.scalar.activation(act2[par], pq[par][:], ACT.Gelu).then_inc(s_a2, 1)

            def norm2(g, par, pairs):
                alone(act, s_pair, pairs)
                wait(act, s_x2T, g)
                for t in range(GT):
                    c = par * GT + t
                    ins = nc.scalar.activation(x2t[par][:, t, :], rowsf[:, bass.ds((g * GT + t) * ROW, D)],
                                               ACT.Identity, bias=nmr[:, c:c + 1], scale=rstd[:, c:c + 1])
                ins.then_inc(s_xn2, 1)

            def x2_copy(g):
                act.wait_ge(s_x2T, g + 1)
                wait(act, s_lg, g)
                nc.scalar.copy(x2f, pe_[0][:]).then_inc(s_x2F, 1)

            queries_gelu(0, 0)

            def recall(i, first, last):
                for par in range(2):
                    g = 2 * i + par
                    if not first:
                        norm2(g - 2, par, i)
                    if not (last and par == 1):
                        queries_gelu(g + 1, 1 - par)
                    if not first:
                        x2_copy(g - 2)
            in_pairs(act, recall, 1)
            for par in range(2):
                norm2(NG - 2 + par, par, NG // 2)
            for par in range(2):
                x2_copy(NG - 2 + par)
            act.wait_ge(s_top, 1)
            nc.scalar.activation(ex, den, ACT.Exp).then_inc(s_rtact, 1)

            act.wait_ge(s_table, 1)

            def norm_rows(a, k, turn):
                act.wait_ge(s_got[k], 16 * (turn + 1))
                wait(act, s_xgT, a - 1)
                nc.scalar.activation(xg[k % 2], got[k][:, 0:D], ACT.Identity, bias=got[k][:, NMR:NMR + 1],
                                     scale=got[k][:, RSTD:RSTD + 1]).then_inc(s_xg, 1)

            norm_rows(0, 0, 0)
            norm_rows(1, 1, 0)

            def experts(i, first, last):
                for k in range(RING):
                    a = RING * i + k
                    if last and a >= NS:
                        continue
                    if not (last and a + 2 >= NS):
                        norm_rows(a + 2, (k + 2) % RING, i + (k + 2) // RING)
                    act.wait_ge(s_u, 2 * a + 1)
                    wait(act, s_hid, a - 1)
                    nc.scalar.copy(u1s[k % 2], (pz, pa)[k % 2][:, 0:F]).then_inc(s_u1, 1)
                    act.wait_ge(s_hid, a + 1)
                    wait(act, s_eaT, a - 1)
                    nc.scalar.activation(act_e[k % 2], hid[k % 2], ACT.Gelu).then_inc(s_ea, 1)
            in_rings(act, experts)

        @block.vector
        def _(dve):
            v = nc.vector
            steps = {}

            def link(ins, s):
                steps[s] = steps.get(s, 0) + 1
                ins.then_inc(s, 1)
                dve.wait_ge(s, steps[s])

            dve.wait_ge(s_pool0, 3)
            v.tensor_scalar(ident[:], colf[:], rowf[:], None, ALU.is_equal)
            v.tensor_scalar(before[:], colf[:], rowf[:], None, ALU.is_gt)
            v.tensor_scalar(lastp[:], rowf[:], float(P - 1), None, ALU.is_equal)
            v.memset(ones_bf[:], 1.0)
            v.memset(tiny_c[:], TINY)
            v.tensor_scalar(rowp1[:], rowf[:], 1.0, None, ALU.add)
            for h in range(GPS):
                for t in range(GT):
                    for half in range(2):
                        c = (h * GT + t) * (P // CHUNK) + half
                        v.memset(decay[half * CHUNK:(half + 1) * CHUNK, h, t:t + 1], GRAD * DECAY ** (NCHUNK - 1 - c))
            v.memset(rows[:, :, SCORE + 1:ROW], 0.0)
            for par in range(2):
                for n in range(NGRAM):
                    lo, hi = (0, 2 if n == 2 else 1) if par == 0 else (GTOK - 1, GTOK)
                    if par == 0 or n > 0:
                        ins = v.memset(embF[par][:, n, lo:hi], 0.0)
            ins.then_inc(s_const, 1)

            def mod(dst, src, done=s_hstep):
                link(v.tensor_scalar(qi, src, 1.0 / VOCAB, None, ALU.mult), s_hstep)
                link(v.scalar_tensor_tensor(rr, qi, -float(VOCAB), src, ALU.mult, ALU.add), s_hstep)
                link(v.tensor_scalar(tt, rr, 0.0, float(VOCAB), ALU.is_lt, ALU.mult), s_hstep)
                link(v.tensor_tensor(rr, rr, tt, ALU.add), s_hstep)
                link(v.tensor_scalar(tt, rr, float(VOCAB), -float(VOCAB), ALU.is_ge, ALU.mult), s_hstep)
                link(v.tensor_tensor(dst, rr, tt, ALU.add), done)

            dve.wait_ge(s_x, 48)
            link(v.tensor_copy(vv, xw), s_hstep)
            mod(hb, vv)
            prev = hb
            for cur in (h2, h3, h4):
                link(v.tensor_copy(vv[:, 0:1], prev[:, 0:1]), s_hstep)
                link(v.scalar_tensor_tensor(vv[:, 1:HW], prev[:, 0:HW - 1], 64.0, hb[:, 1:HW], ALU.mult, ALU.add), s_hstep)
                mod(cur, vv, s_hash if cur is h4 else s_hstep)
                prev = cur
            dve.wait_ge(s_hT, 1)
            v.tensor_copy(idx_all[:], pg[:, 0:NGRAM * NT].rearrange("p (n j) -> p n j", n=NGRAM)).then_inc(s_idx, 1)

            def newton(var, n, g, s, between=None):
                k = [0]
                ve_, se, ya_, yb_, r_ = (t[:, 0:n] for t in (ve, seed, ya, yb, rstd))

                def step(ins):
                    k[0] += 1
                    ins.then_inc(s, 1)
                    dve.wait_ge(s, g * NSTEP + k[0])
                step(v.tensor_scalar(ve_, var, EPS, None, ALU.add))
                step(v.tensor_scalar(se.bitcast(i32), ve_.bitcast(i32), 1, None, ALU.arith_shift_right))
                step(v.tensor_scalar(r_.bitcast(i32), se.bitcast(i32), -1.0, MAGIC, ALU.mult, ALU.add))
                for r in range(3):
                    step(v.scalar_tensor_tensor(ya_, r_, -0.5, ve_, ALU.mult, ALU.mult))
                    step(v.tensor_tensor(yb_, ya_, r_, ALU.mult))
                    step(v.scalar_tensor_tensor(r_, yb_, 1.5, r_, ALU.add, ALU.mult))
                    if r == 0 and between is not None:
                        between()
                assert k[0] == NSTEP

            def bn(g, s_in, s_a, s_b, at_=0):
                alone(dve, s_in, g + 1)
                for t in range(GT):
                    ins = v.bn_stats(stats[:, t, :], rowsf[:, bass.ds((g * GT + t) * ROW, D)])
                ins.then_inc(s_a, 1)
                alone(dve, s_a, g + 1)
                for t in range(GT):
                    ins = v.bn_aggr(mv[:, at_ + t, :], stats[:, t, :])
                ins.then_inc(s_b, 1)
                dve.wait_ge(s_b, g + 1)

            def emb_copy(g, par):
                lo, hi = (1, GTOK) if par == 0 else (0, GTOK - 1)
                dve.wait_ge(s_eT[1], g + 1)
                wait(dve, s_h0, g - 1)
                v.tensor_copy(embF[par][:, 1, lo:hi], pe_[(NGRAM * par + 1) % 2][:, lo:hi]).then_inc(s_eF[1], 1)

            def h0_rows(g):
                dve.wait_ge(s_h0, g + 1)
                v.tensor_tensor(rows[:, bass.ds(g * GT, GT), 0:D], ph[:].rearrange("p (t d) -> p t d", t=GT),
                                bias_bc[:].unsqueeze(1).to_broadcast([P, GT, D]), ALU.add).then_inc(s_h0s, 1)
                bn(g, s_h0s, s_bn, s_ag)

            def norm(g, par):
                wait(dve, s_g0, g - 1)
                for t in range(GT):
                    ins = v.tensor_scalar(xnT[par][:, t, :], rowsf[:, bass.ds((g * GT + t) * ROW, D)],
                                          mv[:, t, 0:1], rstd[:, t:t + 1], ALU.subtract, ALU.mult)
                ins.then_inc(s_xn, 1)

            dve.wait_ge(s_w, 16 * 9)
            emb_copy(0, 0)
            h0_rows(0)
            newton(mv[:, 0:GT, 1], GT, 0, s_nw)
            norm(0, 0)
            zv = pz[:]
            halves = lambda w: w.rearrange("p (h c) -> p h c", h=2)

            def residual(g, par, h):
                dve.wait_ge(s_m, 2 * g + h + 1)
                v.tensor_tensor(res_t[:, h * H:(h + 1) * H].rearrange("p (t d) -> p t d", t=2),
                                pa[:, h * GTOK:h * GTOK + H].rearrange("p (t d) -> p t d", t=2),
                                decay[:, par, 2 * h:2 * h + 2].unsqueeze(2).to_broadcast([P, 2, D]), ALU.mult).then_inc(s_res, 1)

            def slot(g, par, is_first, has1, has2):
                if is_first:
                    emb_copy(1, 1)
                if has1:
                    h0_rows(g + 1)
                dve.wait_ge(s_act, g + 1)
                wait(dve, s_dz, g)
                v.tensor_tensor(num, act_t, zv, ALU.mult).then_inc(s_n1, 1)
                if has1:
                    newton(mv[:, 0:GT, 1], GT, g + 1, s_nw, (lambda: emb_copy(g + 2, par)) if has2 else None)
                wait(dve, s_rT, 2 * g)
                wait(dve, s_g1, g)
                residual(g, par, 0)
                if has1:
                    norm(g + 1, 1 - par)
                residual(g, par, 1)
                dve.wait_ge(s_rT, 2 * g + 2)
                wait(dve, s_da, g)
                v.tensor_copy(halves(res_f[:]), halves(pa[:])[:, :, H:2 * H]).then_inc(s_rF, 1)
                dve.wait_ge(s_n1, g + 1)
                dve.wait_ge(s_r, g + 1)
                v.scalar_tensor_tensor(num, num, TINY / 2, rz2, ALU.add, ALU.mult).then_inc(s_n2, 1)
                dve.wait_ge(s_e, g + 1)
                v.tensor_tensor(ez, ez, zv, ALU.mult).then_inc(s_n3, 1)
                dve.wait_ge(s_n2, g + 1)
                dve.wait_ge(s_n3, g + 1)
                v.scalar_tensor_tensor(num, ez, 1.0 / math.sqrt(2 * math.pi), num, ALU.mult, ALU.add).then_inc(s_gp, 1)
                dve.wait_ge(s_gp, g + 1)
                dve.wait_ge(s_da, g + 1)
                wait(dve, s_g0, g)
                v.tensor_tensor(dz, num, pa[:], ALU.mult).then_inc(s_dz, 1)

            def memory(i, first, last):
                slot(2 * i, 0, first, True, not last)
                slot(2 * i + 1, 1, False, not last, not last)
            in_pairs(dve, memory)

            dve.wait_ge(s_g0, NG)
            dve.wait_ge(s_g1, NG)
            v.tensor_copy(g0raw[:], pg[:, 0:H]).then_inc(s_ups, 1)
            v.tensor_copy(g1T[:], pg[:, H:2 * H]).then_inc(s_ups, 1)
            dve.wait_ge(s_up, 1)
            v.scalar_tensor_tensor(fw0[:], w0_s[:], 1.0 - ALPHA, ph[:, 0:H], ALU.mult, ALU.add).then_inc(s_ups, 1)
            dve.wait_ge(s_up, 2)
            v.scalar_tensor_tensor(fw1[:], w1_s[:], 1.0 - ALPHA, pe_[0][:, 0:H].rearrange("p (c d) -> p c d", c=2),
                                   ALU.mult, ALU.add).then_inc(s_ups, 1)
            dve.wait_ge(s_up, 3)
            v.tensor_copy(wqz[:], pe_[1][:, 0:H]).then_inc(s_ups, 1)

            def logits_copy(g):
                dve.wait_ge(s_lg, g + 1)
                v.tensor_tensor(logits[:, bass.ds(g * GT, GT), :], pe_[1][:, 0:GT * E].rearrange("p (t e) -> p t e", t=GT),
                                br_bc[:].unsqueeze(1).to_broadcast([P, GT, E]), ALU.add).then_inc(s_lgs, 1)

            def recall(i, first, last):
                for par in range(2):
                    g = 2 * i + par
                    dve.wait_ge(s_h1, g + 1)
                    here = rows[:, bass.ds(g * GT, GT), 0:D]
                    v.tensor_tensor(here, ph[:].rearrange("p (t d) -> p t d", t=GT), here, ALU.add).then_inc(s_h1s, 1)
                    bn(g, s_h1s, s_bn2, s_ag2, par * GT)
                    if par == 1:
                        wait(dve, s_xn2, 2 * i)
                        newton(mv[:, :, 1], 2 * GT, i, s_nw2)
                        pair = bass.ds(2 * i * GT, 2 * GT)
                        v.scalar_tensor_tensor(nmr[:], mv[:, :, 0], -1.0, rstd[:], ALU.mult, ALU.mult).then_inc(s_pair, 1)
                        v.tensor_copy(rows[:, pair, RSTD:RSTD + 1], rstd[:].unsqueeze(2))
                        dve.wait_ge(s_pair, i + 1)
                        v.tensor_copy(rows[:, pair, NMR:NMR + 1], nmr[:].unsqueeze(2))
                    if not first:
                        logits_copy(g - 2)
            in_pairs(dve, recall, 1)
            logits_copy(NG - 2)
            logits_copy(NG - 1)

            def b3(a):
                return a.unsqueeze(2).to_broadcast([P, NT, E])

            def red(dst, src, op):
                return v.tensor_reduce(dst, src, AX, op)

            rt = lambda ins: link(ins, s_rt)
            dve.wait_ge(s_lgs, NG)
            dve.wait_ge(s_pool0, 5)
            rt(red(m1, logits[:], ALU.max))
            lg = logits[:]
            for m, t, oh, nxt in ((m1, t0, oh0, lg2), (m2, t1, oh1, None)):
                rt(v.tensor_tensor(eqm, lg, b3(m), ALU.is_equal))
                rt(v.scalar_tensor_tensor(cand, eqm, -float(E), iota_e, ALU.mult, ALU.add))
                rt(red(t, cand, ALU.min))
                rt(v.tensor_tensor(oh, cand, b3(t), ALU.is_equal))
                if nxt is not None:
                    rt(v.scalar_tensor_tensor(nxt, oh, -BIG, lg, ALU.mult, ALU.add))
                    rt(red(m2, nxt, ALU.max))
                    lg = nxt
            link(v.tensor_tensor(den, m2, m1, ALU.subtract), s_top)
            dve.wait_ge(s_rtact, 1)
            rt(v.tensor_scalar(den, ex, 1.0, None, ALU.add))
            rt(v.reciprocal(s0, den))
            rt(v.tensor_tensor(s1, ex, s0, ALU.mult))
            dve.wait_ge(s_cnt, 1)
            rt(v.tensor_reduce(full0, pz[:, 0:fE].rearrange("p (j e) -> p e j", e=E), AX, ALU.add))
            rt(v.tensor_reduce(full1, pz[:, 512:512 + fE].rearrange("p (j e) -> p e j", e=E), AX, ALU.add))
            for full, oh, k in ((full0, oh0, k0), (full1, oh1, k1)):
                rt(v.tensor_scalar(full, full, float(TOK), None, ALU.is_ge))
                rt(v.tensor_tensor(kk, full, oh[:, NT - 1, :], ALU.mult))
                rt(v.tensor_reduce(k, kk, AX, ALU.add))
                rt(v.tensor_tensor(k, k, lastp[:], ALU.mult))
            rt(v.tensor_scalar(imax, t0, float(E), None, ALU.add))
            rt(v.tensor_scalar(pos, t1, float(E), None, ALU.add))
            L = slice(NT - 1, NT)
            for idx, k in ((imax, k0), (pos, k1)):
                rt(v.tensor_scalar(kk[:, 0:1], k, -1.0, 1.0, ALU.mult, ALU.add))
                rt(v.tensor_tensor(idx[:, L], idx[:, L], kk[:, 0:1], ALU.mult))
            rt(v.tensor_tensor(imax, imax, pos, ALU.max))
            link(v.tensor_tensor(ohm, iota_e, b3(imax), ALU.is_equal), s_ohm)
            rt(v.tensor_tensor(kk[:, 0:1], s0[:, L], k0, ALU.mult))
            rt(v.tensor_tensor(kk[:, 1:2], s1[:, L], k1, ALU.mult))
            rt(v.tensor_tensor(cx, kk[:, 0:1], kk[:, 1:2], ALU.add))
            rt(v.tensor_tensor(pos, s0, s1, ALU.add))
            rt(v.tensor_tensor(s0[:, L], s0[:, L], kk[:, 0:1], ALU.subtract))
            rt(v.tensor_tensor(s1[:, L], s1[:, L], kk[:, 1:2], ALU.subtract))
            rt(v.tensor_tensor(pos[:, L], s0[:, L], s1[:, L], ALU.add))
            rt(v.tensor_copy(rows[:, :, SCORE], pos))
            lr = rows[:, NT - 1, :]
            rt(v.scalar_tensor_tensor(lr[:, 0:D], x2t[1][:, GT - 1, :], cx, lr[:, 0:D], ALU.mult, ALU.add))
            rt(v.tensor_scalar(kk[:, 0:1], lr[:, RSTD:RSTD + 1], cx, 1.0, ALU.mult, ALU.add))
            rt(v.reciprocal(kk[:, 1:2], kk[:, 0:1]))
            link(v.tensor_scalar(lr[:, RSTD:NMR + 1], lr[:, RSTD:NMR + 1], kk[:, 1:2], None, ALU.mult), s_rows)
            rt(v.memset(ones_f, 1.0))
            dve.wait_ge(s_rank, 1)
            tot = pa[:, 512:512 + fE].rearrange("p (j e) -> p j e", e=E)
            for e in range(E):
                ins = v.tensor_tensor_scan(incl[:, :, e], ones_f, tot[:, :, e], 0.0, ALU.mult, ALU.add)
            rt(ins)
            rt(v.tensor_scalar(nt_i, incl[:, NT - 1, :], float(P - 1), None, ALU.add))
            rt(v.tensor_scalar(nt_i, nt_i, 7, None, ALU.arith_shift_right))
            rt(v.tensor_copy(nt_f, nt_i))
            rt(v.tensor_tensor_scan(nt_c, ones_f[:, 0:E], nt_f, 0.0, ALU.mult, ALU.add))
            rt(v.tensor_tensor(first, nt_c, nt_f, ALU.subtract))
            rt(v.tensor_scalar(nt_f, first, float(P), None, ALU.mult))
            rt(v.tensor_tensor(base, incl, tot, ALU.subtract))
            rt(v.tensor_tensor(base, base, pa[:, 0:fE].rearrange("p (j e) -> p j e", e=E), ALU.add))
            rt(v.tensor_tensor(base, base, nt_f.unsqueeze(1).to_broadcast([P, NT, E]), ALU.add))
            rt(v.tensor_tensor(base, base, ohm, ALU.mult))
            rt(red(pos, base, ALU.add))
            rt(v.tensor_copy(pos_i, pos))
            rt(v.tensor_scalar(a_i, pos_i, 7, None, ALU.arith_shift_right))
            rt(v.tensor_scalar(b_i, pos_i, P - 1, None, ALU.bitwise_and))
            rt(v.tensor_copy(slot_a, a_i))
            rt(v.tensor_copy(slot_b, b_i))
            wb = colf[:].unsqueeze(1)
            halves = 2
            nh = NT // halves
            for q in range(halves):
                J = slice(q * nh, (q + 1) * nh)
                rt(v.tensor_tensor(oh_a[:, J, :], wb[:, :, 0:NSP].to_broadcast([P, nh, NSP]),
                                   slot_a[:, J].unsqueeze(2).to_broadcast([P, nh, NSP]), ALU.is_equal))
                rt(v.tensor_tensor(val_a[:, J, 0, :], oh_a[:, J, :], tilef[:, J].unsqueeze(2).to_broadcast([P, nh, NSP]), ALU.mult))
                rt(v.tensor_scalar(val_a[:, J, 1, :], oh_a[:, J, :], rowp1[:], None, ALU.mult))
                ins = v.tensor_tensor(oh_b[:, J, :], wb.to_broadcast([P, nh, P]),
                                      slot_b[:, J].unsqueeze(2).to_broadcast([P, nh, P]), ALU.is_equal)
                ins.then_inc(s_onehot, 1)
            rt(v.tensor_tensor(starts, starts, first.unsqueeze(1).to_broadcast([P, NS, E]), ALU.is_ge))
            rt(v.tensor_reduce(tile_e, starts, AX, ALU.add))
            rt(v.tensor_scalar(exp_idx[:, 0:NS], tile_e, -1.0, None, ALU.add))
            dve.wait_ge(s_slots, 1)
            rt(v.tensor_copy(slot_v[:], pe_[0][:, NSP:2 * NSP]))
            rt(v.scalar_tensor_tensor(slot_v[:], pe_[0][:, 0:NSP], float(P), slot_v[:], ALU.mult, ALU.add))
            rt(v.tensor_scalar(slot_idx[:, :, 0], slot_v[:], -1.0, 0.0, ALU.add, ALU.max))
            rt(v.tensor_scalar(val0[:], slot_v[:], 0.0, SKIP, ALU.is_equal, ALU.mult))
            link(v.scalar_tensor_tensor(slot_idx[:, :, 1], slot_v[:], -1.0, val0[:], ALU.add, ALU.add), s_table)

            def in_copy(a, k):
                dve.wait_ge(s_xgT, a + 1)
                wait(dve, s_u, 2 * a - 2)
                v.tensor_copy(xgF[k % 2], ph[:, 0:P]).then_inc(s_xgF, 1)

            def gelu_copy(a, k):
                dve.wait_ge(s_eaT, a + 1)
                wait(dve, s_y, a - 1)
                v.tensor_copy(act_eF[k % 2], pe_[0][:]).then_inc(s_eaF, 1)

            def out_rows(a, k, i):
                dve.wait_ge(s_y, a + 1)
                if isinstance(a, int):
                    wait(dve, s_put[k % 2], 16 * ((a - 2) // 2 + 1))
                else:
                    dve.wait_ge(s_put[k % 2], 16 * (i * (RING // 2) + (k - 2) // 2 + 1))
                r = got[k % RING]
                v.scalar_tensor_tensor(outs[k % 2], pe_[1][:, 0:D], r[:, SCORE:SCORE + 1], r[:, 0:D],
                                       ALU.mult, ALU.add).then_inc(s_o, 1)

            in_copy(0, 0)
            in_copy(1, 1)

            def experts(i, first_, last_):
                for k in range(RING):
                    a = RING * i + k
                    if not (last_ and a >= NS):
                        dve.wait_ge(s_u, 2 * a + 2)
                        dve.wait_ge(s_u1, a + 1)
                        wait(dve, s_ea, a - 1)
                        v.tensor_tensor(hid[k % 2], u1s[k % 2], (pz, pa)[k % 2][:, F:2 * F], ALU.mult).then_inc(s_hid, 1)
                    if not (first_ and k < 1) and not (last_ and a - 1 >= NS):
                        gelu_copy(a - 1, k - 1)
                    if not (last_ and a + 2 >= NS):
                        in_copy(a + 2, k + 2)
                    if not (first_ and k < 2) and not (last_ and a - 2 >= NS):
                        out_rows(a - 2, k - 2, i)
            in_rings(dve, experts)
            n = (NS + RING - 1) // RING
            for a in range(n * RING - 2, NS):
                out_rows(a, a % RING, 0)

        @block.tensor
        def _(pe):
            mm, tr = nc.tensor.matmul, nc.tensor.transpose
            pe.wait_ge(s_const, 1)
            pe.wait_ge(s_w, 16 * 9)
            for n in range(NGRAM):
                tr(pz[:, n * D:(n + 1) * D], proj_s[:, n * D:(n + 1) * D], ident[:])
            tr(pa[:, 0:D], wk_s[:], ident[:])
            tr(pa[:, D:2 * D], wq_s[:], ident[:])
            tr(pa[:, 2 * D:3 * D], w1_s[:, 0, :], ident[:])
            tr(pa[:, 3 * D:4 * D], w1_s[:, 1, :], ident[:]).then_inc(s_wT, 1)
            pe.wait_ge(s_hash, 1)
            tr(pg[:, 0:NT], h2[:, 2:2 + P], ident[0:NT, 0:NT])
            tr(pg[:, NT:2 * NT], h3[:, 3:3 + P], ident[0:NT, 0:NT])
            tr(pg[:, 2 * NT:3 * NT], h4[:, 3:3 + P], ident[0:NT, 0:NT]).then_inc(s_hT, 1)
            pe.wait_ge(s_wTs, 5)
            mm(ph[:, 0:H], wkT[:], w0_s[:], start=True, stop=True).then_inc(s_wkz, 1)
            pe.wait_ge(s_idx, 1)
            pe.wait_ge(s_wkzs, 1)

            def emb_T(g, par, i, which=range(NGRAM)):
                for n in which:
                    pe.wait_ge(s_gath[par][n], 16 * GT * (i + 1))
                    wait(pe, s_eF[(n + 1) % NGRAM], g if n < 2 else g + 1)
                    for t in range(GT):
                        ins = tr(pe_[(NGRAM * par + n) % 2][:, t * P:(t + 1) * P], gath[par][:, n, t, :], ident[:])
                    ins.then_inc(s_eT[n], 1)

            def h0_mm(g, par):
                for n in range(NGRAM):
                    pe.wait_ge(s_eF[n], g + 1)
                wait(pe, s_xF, g)
                for t in range(GT):
                    for n in range(NGRAM):
                        ins = mm(ph[:, t * P:(t + 1) * P], embF[par][:, n, t * P:(t + 1) * P], projT[:, n, :],
                                 start=(n == 0), stop=(n == NGRAM - 1))
                ins.then_inc(s_h0, 1)

            def xn_T(g, par):
                pe.wait_ge(s_xn, g + 1)
                for t in range(GT):
                    ins = tr(ph[:, t * P:(t + 1) * P], xnT[par][:, t, :], ident[:])
                ins.then_inc(s_xT, 1)

            def grad0(g, par, start):
                pe.wait_ge(s_dz, g + 1)
                for t in range(GT):
                    ins = mm(pg[:, 0:H], xnT[par][:, t, :], dz[:, t * H:(t + 1) * H],
                             start=False, stop=False, skip_group_check=True)
                ins.then_inc(s_g0, 1)

            emb_T(0, 0, 0)
            h0_mm(0, 0)
            xn_T(0, 0)

            def slot(g, par, i, is_first, has1, has2):
                pe.wait_ge(s_xF, g + 1)
                wait(pe, s_n3, g)
                for t in range(GT):
                    ins = mm(pz[:, t * H:(t + 1) * H], xnF[par][:, t * P:(t + 1) * P], wkz[:], start=True, stop=True)
                ins.then_inc(s_z, 1)
                if is_first:
                    emb_T(1, 1, 0)
                    h0_mm(1, 1)
                else:
                    grad0(g - 1, 1 - par, False)
                pe.wait_ge(s_act, g + 1)
                for c in range(2):
                    for t in range(GT):
                        ins = tr(pa[:, c * GTOK + t * P:c * GTOK + (t + 1) * P], act_t[:, t * H + c * P:t * H + (c + 1) * P], ident[:])
                ins.then_inc(s_aT, 1)
                if has2:
                    emb_T(g + 2, par, i + 1, (0, 1))
                pe.wait_ge(s_aF, g + 1)
                for h in range(2):
                    for t in (2 * h, 2 * h + 1):
                        T = slice(t * P, (t + 1) * P)
                        to = pa[:, h * GTOK + (t - 2 * h) * P:h * GTOK + (t - 2 * h + 1) * P]
                        mm(to, act_f[:, T], w1_s[:, 0, :], start=True, stop=False)
                        mm(to, act_f[:, GTOK + t * P:GTOK + (t + 1) * P], w1_s[:, 1, :], start=False, stop=False)
                        ins = mm(to, xnF[par][:, T], nwv[:], start=False, stop=True)
                    ins.then_inc(s_m, 1)
                if has2:
                    emb_T(g + 2, par, i + 1, (2,))
                for h in range(2):
                    pe.wait_ge(s_res, 2 * g + h + 1)
                    for t in (2 * h, 2 * h + 1):
                        to = h * GTOK + H + (t - 2 * h) * P
                        ins = tr(pa[:, to:to + P], res_t[:, t * P:(t + 1) * P], ident[:])
                    ins.then_inc(s_rT, 1)
                    for t in (2 * h, 2 * h + 1):
                        one = is_first and t == 0
                        ins = mm(pg[:, H:2 * H], res_t[:, t * P:(t + 1) * P], act_t[:, t * H:(t + 1) * H],
                                 start=one, stop=False, skip_group_check=True)
                ins.then_inc(s_g1, 1)
                if has1:
                    xn_T(g + 1, 1 - par)
                pe.wait_ge(s_rF, g + 1)
                for t in range(GT):
                    ins = mm(pa[:, t * H:(t + 1) * H], res_f[:, t * P:(t + 1) * P], w1T[:], start=True, stop=True)
                ins.then_inc(s_da, 1)
                if has2:
                    h0_mm(g + 2, par)

            def memory(i, first, last):
                slot(2 * i, 0, i, first, True, not last)
                slot(2 * i + 1, 1, i, False, not last, not last)
            in_pairs(pe, memory)
            grad0(NG - 1, 1, False)

            pe.wait_ge(s_ups, 2)
            mm(ph[:, 0:H], wk_s[:], g0raw[:], start=True, stop=True).then_inc(s_up, 1)
            tr(pe_[0][:, 0:D], g1T[:, 0:D], ident[:])
            tr(pe_[0][:, D:H], g1T[:, D:H], ident[:]).then_inc(s_up, 1)
            pe.wait_ge(s_ups, 3)
            mm(pe_[1][:, 0:H], wqT[:], fw0[:], start=True, stop=True).then_inc(s_up, 1)
            pe.wait_ge(s_ups, 5)
            for par in range(2):
                pe.wait_ge(s_xall[par], 16 * (NG // 2))

            pq = [pz, pa]

            def query(g, par):
                wait(pe, s_a2, g - 1)
                for c in range(2):
                    ins = mm(pq[par][:, c * GTOK:(c + 1) * GTOK], wqz[:, c * P:(c + 1) * P],
                             xnF_all[:, bass.ds(g * GTOK, GTOK)], start=True, stop=True)
                ins.then_inc(s_q, 1)

            def x2_T(g, par):
                pe.wait_ge(s_xn2, g + 1)
                wait(pe, s_x2F, g)
                for t in range(GT):
                    ins = tr(pe_[0][:, t * P:(t + 1) * P], x2t[par][:, t, :], ident[:])
                ins.then_inc(s_x2T, 1)

            def logit_mm(g):
                pe.wait_ge(s_x2F, g + 1)
                wait(pe, s_lgs, g)
                for t in range(GT):
                    ins = mm(pe_[1][:, t * E:(t + 1) * E], x2f[:, t * P:(t + 1) * P], wr_s[:], start=True, stop=True)
                ins.then_inc(s_lg, 1)

            query(0, 0)

            def recall(i, first, last):
                for par in range(2):
                    g = 2 * i + par
                    if not (last and par == 1):
                        query(g + 1, 1 - par)
                    if not first:
                        x2_T(g - 2, par)
                    pe.wait_ge(s_a2, g + 1)
                    wait(pe, s_h1s, g)
                    for t in range(GT):
                        for c in range(2):
                            ins = mm(ph[:, t * P:(t + 1) * P], act2[par][:, c * GTOK + t * P:c * GTOK + (t + 1) * P],
                                     fw1[:, c, :], start=(c == 0), stop=(c == 1))
                    ins.then_inc(s_h1, 1)
                    if not first:
                        logit_mm(g - 2)
            in_pairs(pe, recall, 1)
            for par in range(2):
                x2_T(NG - 2 + par, par)
                logit_mm(NG - 2 + par)

            pe.wait_ge(s_top, 1)
            mm(pz[:, 0:fE], ones_bf[:], oh0, start=True, stop=True)
            mm(pz[:, 512:512 + fE], ones_bf[:], oh0, start=True, stop=False)
            mm(pz[:, 512:512 + fE], ones_bf[:], oh1, start=False, stop=True).then_inc(s_cnt, 1)
            pe.wait_ge(s_ohm, 1)
            mm(pa[:, 0:fE], before[:], ohm, start=True, stop=True)
            mm(pa[:, 512:512 + fE], ones_bf[:], ohm, start=True, stop=True).then_inc(s_rank, 1)
            for j in range(NT):
                if j % (NT // 2) == 0:
                    pe.wait_ge(s_onehot, j // (NT // 2) + 1)
                ins = mm(pe_[0][:, 0:2 * NSP], oh_b[:, j, :], val_a[:, j, :, :].rearrange("p v a -> p (v a)"),
                         start=(j == 0), stop=(j == NT - 1))
            ins.then_inc(s_slots, 1)

            pe.wait_ge(s_f, 48)
            pe.wait_ge(s_table, 1)

            def in_T(a, k):
                pe.wait_ge(s_xg, a + 1)
                wait(pe, s_xgF, a)
                tr(ph[:, 0:P], xg[k % 2], ident[:]).then_inc(s_xgT, 1)

            def expert_of(a):
                return pe.value_load(exp_idx[0:1, bass.ds(a, 1)], min_val=0, max_val=E - 1)

            def down(a, k, e):
                pe.wait_ge(s_eaF, a + 1)
                wait(pe, s_o, a)
                for c in range(4):
                    ins = mm(pe_[1][:, 0:D], act_eF[k % 2][:, c * P:(c + 1) * P], f3_f[:, bass.ds(e * F + c * D, D)],
                             start=(c == 0), stop=(c == 3))
                ins.then_inc(s_y, 1)

            def gelu_T(a, k):
                pe.wait_ge(s_ea, a + 1)
                wait(pe, s_eaF, a)
                for c in range(4):
                    ins = tr(pe_[0][:, c * P:(c + 1) * P], act_e[k % 2][:, c * P:(c + 1) * P], ident[:])
                ins.then_inc(s_eaT, 1)

            in_T(0, 0)
            in_T(1, 1)

            def experts(i, first, last):
                e = {0: expert_of(RING * i)}
                for k in range(RING):
                    a = RING * i + k
                    if not (last and a >= NS):
                        pu = (pz, pa)[k % 2]
                        pe.wait_ge(s_xgF, a + 1)
                        wait(pe, s_hid, a - 1)
                        mm(pu[:, 0:F], xgF[k % 2], f2_f[:, bass.ds(e[k] * F, F)], start=True, stop=True).then_inc(s_u, 1)
                        mm(pu[:, F:2 * F], xgF[k % 2], f1_f[:, bass.ds(e[k] * F, F)], start=True, stop=True).then_inc(s_u, 1)
                    if k + 1 < RING and not (last and a + 1 >= NS):
                        e[k + 1] = expert_of(a + 1)
                    if k == 0 and not first:
                        e[-2], e[-1] = expert_of(a - 2), expert_of(a - 1)
                    if not (last and a + 2 >= NS):
                        in_T(a + 2, k + 2)
                    if not (first and k < 1) and not (last and a - 1 >= NS):
                        gelu_T(a - 1, k - 1)
                    if not (first and k < 2) and not (last and a - 2 >= NS):
                        down(a - 2, k - 2, e[k - 2])
            in_rings(pe, experts)
            n = (NS + RING - 1) // RING
            for a in range(n * RING - 2, NS):
                down(a, a, expert_of(a))


_INS = ['x', 'L0_tok_emb_2', 'L0_tok_emb_3', 'L0_tok_emb_4', 'L0_tok_proj_w', 'L0_tok_proj_b', 'L0_attn_w_k',
        'L0_attn_w_v', 'L0_attn_w_q', 'L0_attn_W0', 'L0_attn_W1', 'L0_ffn_Wr', 'L0_ffn_br', 'L0_ffn_W1',
        'L0_ffn_W2', 'L0_ffn_W3']
_OUTS = [((BATCH, SEQ, D), 'float32')]


def kernel(**inputs):
    import numpy as _np
    import concourse.bacc as _bacc
    from concourse import mybir as _mybir
    from concourse.bass_utils import run_bass_kernel_spmd as _run

    nc = _bacc.Bacc("TRN2", target_bir_lowering=False, num_devices=1)
    arrays, args = {}, []
    for name in _INS:
        a = _np.ascontiguousarray(inputs[name])
        arrays[f"in_{name}_dram"] = a
        args.append(nc.dram_tensor(f"in_{name}_dram", a.shape, _mybir.dt.from_np(a.dtype), kind="ExternalInput").ap())
    for i, (shape, dtype) in enumerate(_OUTS):
        dt = _mybir.dt.from_np(_np.dtype(dtype))
        args.append(nc.dram_tensor(f"out_{i}_dram", shape, dt, kind="ExternalOutput").ap())
    tower(nc, *args)
    r = _run(nc, [arrays], core_ids=[0])
    return r.results[0]["out_0_dram"]
```

```python
import math
from contextlib import ExitStack

import concourse.bass as bass
from concourse import mybir

P = 128
BATCH, SEQ = 8, 1024
TOK = BATCH * SEQ
D = 128
H = 256
F = 512
E = 8
NGRAM = 3
VOCAB = 25000
CHUNK = 64
NCHUNK = SEQ // CHUNK
NT = TOK // P
GT = 4
GTOK = GT * P
NG = TOK // GTOK
GPS = SEQ // GTOK
NS = NT + E - 1
GROW = 132
RSTD, NMR, SCORE = 128, 129, 130
HB = E
ROW = HB + GROW
EXT = HB + D
RING = 8
WPARTS = 8
WCOLS = 2 * E * F // WPARTS
PART = 16
LAG = 6
ALPHA, LR, DECAY = 0.1, 0.01, 0.9
EPS = 1e-5
TINY = 2.0 ** -60
GRAD = -LR * 2.0 / (BATCH * CHUNK * D)
MAGIC = float(0x5F3759DF)
SKIP = float(1 << 20)
BIG = 3.0e38


def wait(eng, sem, value):
    if isinstance(value, int) and value <= 0:
        return
    eng.wait_ge(sem, value)


def tower(nc, x, emb2, emb3, emb4, proj_w, proj_b, w_k, w_v, w_q, W0, W1, Wr, br, F1, F2, F3, out):
    f32, bf16, i32 = mybir.dt.float32, mybir.dt.bfloat16, mybir.dt.int32
    f32r = mybir.dt.float32r
    ALU, ACT, AX = mybir.AluOpType, mybir.ActivationFunctionType, mybir.AxisListType.X
    tables = [emb2, emb3, emb4]
    ctx = ExitStack()
    with ctx:
        def sb(name, shape, dt=f32):
            return ctx.enter_context(nc.sbuf_tensor(name, shape, dt))

        def sem(name):
            return ctx.enter_context(nc.semaphore(name))

        colf = sb("colf", [P, P])
        colb = sb("colb", [P, P], bf16)
        rowf = sb("rowf", [P, 1])
        ident = sb("ident", [P, P])
        before = sb("before", [P, P], bf16)
        iota_m = sb("iota_m", [P, E])
        ones_bf = sb("ones_bf", [P, P], bf16)
        decay = sb("decay", [P, GPS, GT])
        lastp = sb("lastp", [P, 1])
        tiny_c = sb("tiny_c", [P, 1])
        gelu_zero = sb("gelu_zero", [P, 1])
        rowp1 = sb("rowp1", [P, 1])
        proj_s = sb("proj_s", [P, NGRAM * D])
        projT = sb("projT", [P, NGRAM, EXT])
        bias_bc = sb("bias_bc", [P, EXT])
        br_bc = sb("br_bc", [P, E])
        wr_sum = sb("wr_sum", [P, E])
        wk_s, wv_s, wq_s = sb("wk_s", [P, D]), sb("wv_s", [P, D]), sb("wq_s", [P, D])
        wkT, wqT, nwv = sb("wkT", [P, D]), sb("wqT", [P, D]), sb("nwv", [P, D])
        w0_s = sb("w0_s", [P, H])
        w1_s = sb("w1_s", [P, 2, D])
        w1T = sb("w1T", [P, H])
        wkz = sb("wkz", [P, H])
        g0raw = sb("g0raw", [P, H])
        fw1T = sb("fw1T", [P, H])
        fw0 = sb("fw0", [P, H])
        fw1 = sb("fw1", [P, 2, EXT])
        wqz = sb("wqz", [P, H])
        wr_s = sb("wr_s", [P, E])
        with nc.sbuf_tensor("xnF_all", [P, TOK], f32) as xnF_all, nc.sbuf_tensor("up_w", [P, 2 * E * F], f32) as up_w:
            pass
        up_h = sb("up_h", [P, 2 * E * F], f32r)
        up_l = sb("up_l", [P, 2 * E * F], f32r)
        f3_s = sb("f3_s", [P, E, 4, D])
        f3_f = f3_s[:].rearrange("p e c d -> p (e c d)")
        rows = sb("rows", [P, NT, ROW])
        rowsf = rows[:].rearrange("p j c -> p (j c)")
        logits = sb("logits", [P, NT, E])
        work = sb("work", [P, 16384])
        at = [0]

        def carve(cols, dt=f32):
            a = at[0]
            at[0] += cols
            assert at[0] <= 16384, at[0]
            v = work[:, a:a + cols]
            return v if dt is f32 else v.bitcast(dt)

        gath = [carve(NGRAM * GTOK).rearrange("p (n t d) -> p n t d", n=NGRAM, t=GT) for _ in range(2)]
        embF = [carve(NGRAM * GTOK).rearrange("p (n c) -> p n c", n=NGRAM) for _ in range(2)]
        xnT = [carve(GTOK).rearrange("p (t d) -> p t d", t=GT) for _ in range(2)]
        xnF = [carve(GTOK) for _ in range(2)]
        act_t = carve(GT * H)
        act_f = carve(2 * GTOK)
        zsq, rz2, ez = (carve(GT * H) for _ in range(3))
        lnz = rz2
        num = carve(GT * H)
        late_at = at[0]
        dz = carve(GT * H)
        res_t = carve(GTOK)
        res_f = sb("res_f", [P, GTOK])
        idx_all = sb("idx_all", [P, NGRAM, NT], i32)
        idx_g = [sb(f"idx_g{k}", [P, NGRAM, GT], i32) for k in range(2)]
        stats, mv = sb("stats", [P, GT, 6]), sb("mv", [P, 2 * GT, 2])
        ve, seed, ya, yb, rstd = (sb(n, [P, 2 * GT]) for n in ("ve", "seed", "ya", "yb", "rstd"))
        nmr, nmean, minus_half = (sb(n, [P, 2 * GT]) for n in ("nmr", "nmean", "minus_half"))
        at[0] = 0
        lg_a, lg_b = (carve(2 * GT * E).rearrange("p (t e) -> p t e", e=E) for _ in range(2))
        route_at = at[0]
        act2 = [carve(2 * GTOK) for _ in range(2)]
        at[0] = route_at
        fE = NT * E
        x_last = carve(D)
        big3 = lambda v: v.rearrange("p (j e) -> p j e", e=E)
        oh_a_at = at[0]
        eqm, cand, lg2 = big3(carve(fE)), big3(carve(fE)), big3(carve(fE))
        oh01 = carve(fE, bf16).rearrange("p (j v e) -> p j v e", v=2, e=E)
        ohm = big3(carve(fE // 2, bf16))
        incl, base = big3(carve(fE)), big3(carve(fE))
        m1, m2, imax, ex, den, s0, s1, pos = (carve(NT) for _ in range(8))
        t01 = carve(2 * NT).rearrange("p (j v) -> p j v", v=2)
        slot_a, slot_b = (carve(NT // 2, bf16) for _ in range(2))
        pos_i, a_i, b_i = (carve(NT, i32) for _ in range(3))
        ones_f = carve(NT)
        cnt_a, cnt_b, full, kk = (carve(2 * E) for _ in range(4))
        cnt = carve(E, bf16)
        drop, stay, both, gone, cx, sc = carve(2), carve(2), carve(2), carve(2), carve(1), carve(2)
        score, grow, shrink, rest = carve(NT), carve(1), carve(1), carve(1)
        nt_f, nt_i, nt_c, first = carve(E), carve(E, i32), carve(E), carve(E)
        starts = carve(NS * E).rearrange("p (a e) -> p a e", e=E)
        tile_e = carve(NS)
        NSP = NS + 1
        oh_b = carve(NT * P // 2, bf16).rearrange("p (j b) -> p j b", b=P)
        val_a = carve(NT * NSP, bf16).rearrange("p (j v a) -> p j v a", v=2, a=NSP)
        oh_a = work[:, oh_a_at:oh_a_at + NT * NSP // 2].bitcast(bf16).rearrange("p (j a) -> p j a", a=NSP)
        assert NT * NSP // 2 <= 5 * fE
        slot_v = sb("slot_v", [P, NSP])
        val0 = sb("val0", [P, NSP])
        slot_idx = sb("slot_idx", [P, NSP, 2], i32)
        slot_if = slot_idx[:].rearrange("p a v -> p (a v)")
        exp_idx = sb("exp_idx", [P, NSP], i32)
        at[0] = 0
        got = [carve(GROW) for k in range(RING)]
        idx_s = [sb(f"idx_s{k}", [P, 2], i32) for k in range(RING)]
        xg = [carve(P) for _ in range(2)]
        xg_h, xg_l = ([sb(f"xg_{w}{k}", [P, P], f32r) for k in range(2)] for w in "hl")
        u1s = [carve(F) for _ in range(2)]
        hid = [carve(F) for _ in range(2)]
        act_e = [carve(F) for _ in range(2)]
        act_eF = [carve(F) for _ in range(2)]
        outs = [carve(P) for _ in range(2)]
        HW = P + 3
        at[0] = late_at
        xw = carve(HW, i32)[0:NT]
        hb, h2, h3, h4, vv, rr, tt = (carve(HW)[0:NT] for _ in range(7))
        qi = carve(HW, i32)[0:NT]
        biasT, ones_w = carve(P), carve(P)
        assert at[0] <= late_at + GT * H + GTOK
        pz = ctx.enter_context(nc.psum_tensor("pz", [P, 1024], f32))
        pa = ctx.enter_context(nc.psum_tensor("pa", [P, 1024], f32))
        pe_ = [ctx.enter_context(nc.psum_tensor(f"pe{k}", [P, 512], f32)) for k in range(2)]
        ph = ctx.enter_context(nc.psum_tensor("ph", [P, 512], f32))
        pg = ctx.enter_context(nc.psum_tensor("pg", [P, 512], f32))
        rows_d = nc.dram_tensor("rows_d", (TOK, GROW), f32).ap()

        s_x, s_w, s_f, s_row = sem("x_loaded"), sem("weights_loaded"), sem("experts_loaded"), sem("rows_stored")
        s_const, s_pool0, s_hz = sem("constants_made"), sem("iotas_made"), sem("x_zeroed")
        s_hstep, s_hash = sem("hash_step"), [sem(f"hash_made{n}") for n in range(NGRAM)]
        s_hT, s_idx = sem("hashes_transposed"), sem("indices_made")
        s_wT, s_wTs, s_wkz, s_wkzs = sem("weights_transposed"), sem("weight_copies"), sem("wkz_in_psum"), sem("wkz_made")
        s_icopy = [sem(f"group_indices{k}") for k in range(2)]
        s_gath = [[sem(f"gathered{k}_{n}") for n in range(NGRAM)] for k in range(2)]
        s_eT = [sem(f"embedding_transposed{n}") for n in range(NGRAM)]
        s_eF = [sem(f"embedding_copied{n}") for n in range(NGRAM)]
        s_h0, s_h0s = sem("h0_in_psum"), sem("h0_copied")
        s_bn, s_ag, s_nw, s_xn = sem("stats_made"), sem("stats_joined"), sem("newton_step"), sem("normed")
        s_xT, s_xF, s_xall = sem("normed_transposed"), sem("normed_copied"), [sem(f"normed_kept{k}") for k in range(2)]
        s_z, s_act, s_sq, s_ln, s_r, s_e = (sem(n) for n in ("z_in_psum", "gelu_made", "z_squared", "log_made", "inverse_made", "exp_made"))
        s_aT, s_aF = sem("gelu_transposed"), sem("gelu_copied")
        s_m, s_res, s_rT, s_rF, s_g1 = (sem(n) for n in ("residual_in_psum", "residual_made", "residual_transposed", "residual_copied", "grad1_added"))
        s_n1, s_n2, s_n3, s_gp = (sem(n) for n in ("gz_made", "phi_made", "ez_made", "slope_made"))
        s_da, s_dz, s_g0 = sem("da_in_psum"), sem("dz_made"), sem("grad0_added")
        s_up, s_ups = sem("update_in_psum"), sem("update_copied")
        s_q, s_a2, s_h1, s_h1s = sem("zq_in_psum"), sem("gelu2_made"), sem("h1_in_psum"), sem("h1_copied")
        s_mvu, s_scaled = sem("pair_stats_used"), sem("scales_in_rows")
        s_bn2, s_ag2, s_nw2 = (sem(n) for n in ("stats2_made", "stats2_joined", "newton2_step"))
        s_raw, s_lgs = sem("logit_term_made"), sem("logits_made")
        s_rt, s_cready, s_top, s_rtact, s_cnt, s_rank, s_ohm, s_rows = (sem(n) for n in (
            "route_step", "choices_summed", "top_two_found", "score_exp", "choices_counted", "ranks_in_psum", "choice_ready", "rows_ready"))
        s_stay, s_s0, s_score = sem("drops_found"), sem("first_scores_made"), sem("score_step")
        s_oha, s_val = sem("tile_one_hots_made"), sem("tile_numbers_made")
        s_onehot, s_slots, s_table = sem("one_hots_made"), sem("slots_in_psum"), sem("slot_table_made")
        s_is = sem("slot_indices_copied")
        s_got = [sem(f"rows_gathered{k}") for k in range(RING)]
        s_put = [sem(f"rows_scattered{k}") for k in range(2)]
        s_wh, s_wl = sem("expert_weights_high"), sem("expert_weights_low")
        s_xgH = sem("expert_in_high")
        s_xg, s_xgT, s_xgF = sem("expert_in_normed"), sem("expert_in_transposed"), sem("expert_in_copied")
        s_u, s_u1, s_hid, s_ea, s_eaT, s_eaF = (sem(n) for n in ("up_in_psum", "up1_copied", "hidden_made", "expert_gelu", "expert_gelu_transposed", "expert_gelu_copied"))
        s_y, s_o = sem("expert_out_in_psum"), sem("expert_out_made")

        def alone(eng, sem, value):
            if not isinstance(value, int):
                value = eng.to_reg(value)
            eng.wait_ge(s_const, 1)
            eng.wait_ge(sem, value)

        NSTEP = 12
        POOL_STEPS = 10
        block = ctx.enter_context(nc.Block())

        def in_pairs(eng, body):
            body(0, True, False)
            with eng.Fori(1, NG // 2 - 1) as i:
                body(i, False, False)
            body(NG // 2 - 1, False, True)

        def in_rings(eng, body):
            n = (NS + RING - 1) // RING
            body(0, True, False)
            with eng.Fori(1, n - 1) as i:
                body(i, False, False)
            body(n - 1, False, True)

        @block.sync
        def _(sp):
            xt = x.rearrange("b (j p) -> (b j) p", p=P)
            sp.wait_ge(s_hz, 1)
            sp.dma_start(xw[:, 2:2 + P], xt).then_inc(s_x, 16)
            sp.dma_start(xw[1:NT, 0:2], xt[0:NT - 1, P - 2:P]).then_inc(s_x, 16)
            sp.dma_start(xw[0:NT - 1, 2 + P:3 + P], xt[1:NT, 0:1], allow_slow_non_contiguous=True).then_inc(s_x, 16)
            for dst, src in ((proj_s[:], proj_w), (wk_s[:], w_k), (wv_s[:], w_v), (wq_s[:], w_q), (w0_s[:], W0),
                             (w1_s[:], W1.rearrange("(c p) d -> p c d", p=P)), (wr_s[:], Wr),
                             (bias_bc[:, HB:EXT], proj_b[None, :].to_broadcast([P, D])),
                             (br_bc[:], br[None, :].to_broadcast([P, E]))):
                sp.dma_start(dst, src).then_inc(s_w, 16)

            def keep(i, first, last):
                for par in range(2):
                    g = 2 * i + par
                    sp.wait_ge(s_xF, g + 1)
                    sp.dma_start(xnF_all[:, bass.ds(g * GTOK, GTOK)], xnF[par]).then_inc(s_xall[par], 16)
            in_pairs(sp, keep)
            sp.dma_start(up_w[:, E * F:2 * E * F].rearrange("p (e f) -> p e f", e=E), F1.rearrange("e p f -> p e f")).then_inc(s_f, 16)
            sp.dma_start(up_w[:, 0:E * F].rearrange("p (e f) -> p e f", e=E), F2.rearrange("e p f -> p e f")).then_inc(s_f, 16)
            sp.dma_start(f3_s[:], F3.rearrange("e (c p) d -> p e c d", p=P)).then_inc(s_f, 16)
            rows_t = rows_d.rearrange("(j p) c -> p j c", p=P)
            sp.wait_ge(s_rows, 1)
            sp.dma_start(rows_t[:, 0:NT - 1, :], rows[:, 0:NT - 1, HB:ROW]).then_inc(s_row, 16)
            sp.wait_ge(s_rows, 2)
            sp.dma_start(rows_t[:, NT - 1, :], rows[:, NT - 1, HB:ROW]).then_inc(s_row, 16)

        @block.gpsimd
        def _(pool):
            nc.gpsimd.memset(xw[:], 0).then_inc(s_hz, 1)
            nc.gpsimd.iota(colf[:], pattern=[[1, P]], base=0, channel_multiplier=0,
                           allow_small_or_imprecise_dtypes=True).then_inc(s_pool0, 1)
            nc.gpsimd.iota(rowf[:], pattern=[[0, 1]], base=0, channel_multiplier=1,
                           allow_small_or_imprecise_dtypes=True).then_inc(s_pool0, 1)

            def gathers(i, first, last):
                for par in range(2):
                    g = 2 * i + par
                    for n in range(NGRAM):
                        wait(pool, s_eT[n], g - 1)
                    if not (first and par == 0):
                        pool.wait_ge(s_idx, NGRAM)
                        nc.gpsimd.tensor_copy(idx_g[par][:], idx_all[:, :, bass.ds(g * GT, GT)]).then_inc(s_icopy[par], 1)
                        alone(pool, s_icopy[par], i + (NGRAM if par == 0 else 1))
                    for n in range(NGRAM):
                        if first and par == 0:
                            pool.wait_ge(s_idx, n + 1)
                            nc.gpsimd.tensor_copy(idx_g[0][:, n, :], idx_all[:, n, 0:GT]).then_inc(s_icopy[0], 1)
                            alone(pool, s_icopy[0], n + 1)
                        for t in range(GT):
                            nc.gpsimd.indirect_dma_start(
                                out=gath[par][:, n, t, :], out_offset=None, in_=tables[n],
                                in_offset=bass.IndirectOffsetOnAxis(ap=idx_g[par][:, n, t:t + 1], axis=0),
                            ).then_inc(s_gath[par][n], 16)
            in_pairs(pool, gathers)

            def pair_logits(i, first, last):
                alone(pool, s_ag2, 2 * i + 2)
                k = [0]

                def step(ins):
                    k[0] += 1
                    ins.then_inc(s_nw2, 1)
                    alone(pool, s_nw2, i * POOL_STEPS + k[0])
                nc.gpsimd.tensor_scalar(nmean[:], mv[:, :, 0], -1.0, None, ALU.mult).then_inc(s_mvu, 1)
                nc.gpsimd.tensor_scalar(ve[:], mv[:, :, 1], EPS, None, ALU.add).then_inc(s_mvu, 1)
                alone(pool, s_mvu, 2 * i + 2)
                step(nc.gpsimd.tensor_tensor(rstd[:], ve[:], minus_half[:], ALU.pow))
                for _ in range(2):
                    step(nc.gpsimd.tensor_tensor(ya[:], rstd[:], rstd[:], ALU.mult))
                    step(nc.gpsimd.tensor_tensor(yb[:], ya[:], ve[:], ALU.mult))
                    step(nc.gpsimd.tensor_scalar(ya[:], yb[:], -0.5, 1.5, ALU.mult, ALU.add))
                    step(nc.gpsimd.tensor_tensor(rstd[:], rstd[:], ya[:], ALU.mult))
                step(nc.gpsimd.tensor_tensor(nmr[:], nmean[:], rstd[:], ALU.mult))
                assert k[0] == POOL_STEPS
                pair = bass.ds(2 * i * GT, 2 * GT)
                over = lambda a: a.unsqueeze(2).to_broadcast([P, 2 * GT, E])
                alike = lambda a: a.unsqueeze(1).to_broadcast([P, 2 * GT, E])
                nc.gpsimd.tensor_tensor(lg_a, rows[:, pair, 0:E], over(rstd[:]), ALU.mult).then_inc(s_raw, 1)
                nc.gpsimd.tensor_tensor(lg_b, alike(wr_sum[:]), over(nmr[:]), ALU.mult).then_inc(s_raw, 1)
                alone(pool, s_raw, 3 * i + 2)
                nc.gpsimd.tensor_tensor(lg_a, lg_a, lg_b, ALU.add).then_inc(s_raw, 1)
                alone(pool, s_raw, 3 * i + 3)
                nc.gpsimd.tensor_tensor(logits[:, pair, :], lg_a, alike(br_bc[:]), ALU.add).then_inc(s_lgs, 1)
                nc.gpsimd.tensor_copy(rows[:, pair, HB + RSTD:HB + RSTD + 1], rstd[:].unsqueeze(2)).then_inc(s_scaled, 1)
                nc.gpsimd.tensor_copy(rows[:, pair, HB + NMR:HB + NMR + 1], nmr[:].unsqueeze(2)).then_inc(s_scaled, 1)
            in_pairs(pool, pair_logits)

            def scores():
                k = [0]

                def step(ins):
                    k[0] += 1
                    ins.then_inc(s_score, 1)
                    alone(pool, s_score, k[0])
                tt, ts = nc.gpsimd.tensor_tensor, nc.gpsimd.tensor_scalar
                L = slice(NT - 1, NT)
                pool.wait_ge(s_stay, 1)
                pool.wait_ge(s_s0, 1)
                step(tt(s1, ex, s0, ALU.mult))
                step(tt(score, s0, s1, ALU.add))
                alone(pool, s_scaled, NG)
                nc.gpsimd.tensor_copy(rows[:, 0:NT - 1, HB + SCORE:HB + SCORE + 1],
                                      score[:, 0:NT - 1].unsqueeze(2)).then_inc(s_rows, 1)
                lr = rows[:, NT - 1, HB:ROW]
                wide = lambda a: a.to_broadcast([P, D])
                step(nc.gpsimd.tensor_copy(sc[:, 0:1], s0[:, L]))
                step(nc.gpsimd.tensor_copy(sc[:, 1:2], s1[:, L]))
                step(tt(gone, sc, drop, ALU.mult))
                step(tt(cx, gone[:, 0:1], gone[:, 1:2], ALU.add))
                step(tt(sc, sc, stay, ALU.mult))
                step(tt(lr[:, SCORE:SCORE + 1], sc[:, 0:1], sc[:, 1:2], ALU.add))
                step(tt(x_last, lr[:, 0:D], wide(lr[:, RSTD:RSTD + 1]), ALU.mult))
                step(tt(x_last, x_last, wide(lr[:, NMR:NMR + 1]), ALU.add))
                step(tt(x_last, x_last, wide(cx), ALU.mult))
                step(tt(lr[:, 0:D], lr[:, 0:D], x_last, ALU.add))
                step(tt(grow, lr[:, RSTD:RSTD + 1], cx, ALU.mult))
                step(ts(grow, grow, 1.0, None, ALU.add))
                step(tt(shrink, grow, minus_half[:, 0:1], ALU.pow))
                step(tt(shrink, shrink, shrink, ALU.mult))
                step(tt(rest, shrink, grow, ALU.mult))
                step(ts(rest, rest, -1.0, 2.0, ALU.mult, ALU.add))
                step(tt(shrink, shrink, rest, ALU.mult))
                nc.gpsimd.tensor_tensor(lr[:, RSTD:NMR + 1], lr[:, RSTD:NMR + 1], shrink.to_broadcast([P, 2]),
                                        ALU.mult).then_inc(s_rows, 1)

            for c in range(WPARTS):
                C = slice(c * WCOLS, (c + 1) * WCOLS)
                if c == 3:
                    scores()
                pool.wait_ge(s_wh, c + 1)
                nc.gpsimd.tensor_tensor(up_l[:, C], up_w[:, C], up_h[:, C].bitcast(f32), ALU.subtract).then_inc(s_wl, 1)
            pool.wait_ge(s_table, 1)
            pool.wait_ge(s_row, 32)

            def gather(a, k, i):
                if not (isinstance(a, int) and a < RING):
                    pool.wait_ge(s_put[k % 2], 16 * ((a - RING) // 2 + 1) if isinstance(a, int)
                                 else 16 * (i * (RING // 2) + (k - RING) // 2 + 1))
                nc.gpsimd.tensor_copy(idx_s[k][:], slot_if[:, bass.ds(2 * a, 2)]).then_inc(s_is, 1)
                alone(pool, s_is, a + 1)
                nc.gpsimd.indirect_dma_start(
                    out=got[k], out_offset=None, in_=rows_d,
                    in_offset=bass.IndirectOffsetOnAxis(ap=idx_s[k][:, 0:1], axis=0)).then_inc(s_got[k], 16)

            def scatter(a, k):
                alone(pool, s_o, a + 1)
                nc.gpsimd.indirect_dma_start(
                    out=out.rearrange("b s d -> (b s) d"), in_=outs[k % 2],
                    out_offset=bass.IndirectOffsetOnAxis(ap=idx_s[k][:, 1:2], axis=0), in_offset=None,
                    bounds_check=TOK - 1, oob_is_err=False).then_inc(s_put[k % 2], 16)

            def move(i, first, last):
                for k in range(RING):
                    a = RING * i + k
                    if not (last and a >= NS):
                        gather(a, k, i)
                    if not (first and k < LAG):
                        scatter(a - LAG, (k - LAG) % RING)
            in_rings(pool, move)
            n = (NS + RING - 1) // RING
            for a in range(n * RING - LAG, NS):
                scatter(a, a % RING)
            for par in range(2):
                pool.wait_ge(s_put[par], 16 * ((NS - par + 1) // 2))

        @block.scalar
        def _(act):
            def indices(n):
                act.wait_ge(s_hT, n + 1)
                nc.scalar.copy(idx_all[:, n, :], hT[n][:, 0:NT]).then_inc(s_idx, 1)

            hT = (pg, pe_[0], pe_[1])
            indices(0)
            act.wait_ge(s_w, 16 * 9)
            nc.scalar.mul(nwv[:], wv_s[:], -1.0).then_inc(s_wTs, 1)
            indices(1)
            act.wait_ge(s_wT, 1)
            nc.scalar.copy(projT[:, :, HB:EXT], pz[:, 0:NGRAM * D].rearrange("p (n d) -> p n d", n=NGRAM)).then_inc(s_wTs, 1)
            nc.scalar.copy(projT[:, :, 0:E], pz[:, NGRAM * D:NGRAM * (D + E)].rearrange("p (n e) -> p n e", n=NGRAM)).then_inc(s_wTs, 1)
            nc.scalar.copy(biasT, pa[:, GTOK:GTOK + P]).then_inc(s_wTs, 1)
            nc.scalar.copy(wkT[:], pa[:, 0:D]).then_inc(s_wTs, 1)
            nc.scalar.copy(wqT[:], pa[:, D:2 * D]).then_inc(s_wTs, 1)
            indices(2)
            nc.scalar.copy(w1T[:], pa[:, 2 * D:2 * D + H]).then_inc(s_wTs, 1)
            act.wait_ge(s_wkz, 1)
            nc.scalar.copy(wkz[:], ph[:, 0:H])
            nc.scalar.copy(bias_bc[:, 0:E], ph[:, H:H + E])
            nc.scalar.copy(wr_sum[:], ph[:, H + E:H + 2 * E]).then_inc(s_wkzs, 1)

            def emb_copy(g, par, n):
                lo = (0 if par else 1 if n < 2 else 2)
                hi = GTOK - (1 if par and n > 0 else 0)
                act.wait_ge(s_eT[n], g + 1)
                wait(act, s_h0, g - 1)
                nc.scalar.copy(embF[par][:, n, lo:hi], pe_[(NGRAM * par + n) % 2][:, lo:hi]).then_inc(s_eF[n], 1)

            def normed_copy(g, par, i):
                act.wait_ge(s_xT, g + 1)
                wait(act, s_m, 2 * (g - 1))
                wait(act, s_xall[par], 16 * i)
                nc.scalar.copy(xnF[par], ph[:]).then_inc(s_xF, 1)

            act.wait_ge(s_const, 1)
            emb_copy(0, 0, 0)
            emb_copy(0, 0, 2)
            normed_copy(0, 0, 0)

            def slot(g, par, i, is_first, late, has1, has2):
                act.wait_ge(s_z, g + 1)
                wait(act, s_aT, g)
                wait(act, s_g1, g)
                nc.scalar.activation(act_t, pz[:], ACT.Gelu).then_inc(s_act, 1)
                if is_first:
                    emb_copy(1, 1, 0)
                if has2 and not late:
                    emb_copy(g + 2, par, 0)
                act.wait_ge(s_aT, g + 1)
                wait(act, s_m, 2 * g)
                nc.scalar.copy(act_f, pa[:]).then_inc(s_aF, 1)
                if is_first:
                    emb_copy(1, 1, 2)
                act.wait_ge(s_n1, g + 1)
                nc.scalar.activation(zsq, pz[:], ACT.Square).then_inc(s_sq, 1)
                act.wait_ge(s_sq, g + 1)
                wait(act, s_gp, g)
                nc.scalar.activation(lnz, zsq, ACT.Ln, bias=tiny_c[:]).then_inc(s_ln, 1)
                if late:
                    emb_copy(g + 2, par, 0)
                elif has2:
                    emb_copy(g + 2, par, 2)
                act.wait_ge(s_ln, g + 1)
                nc.scalar.activation(rz2, lnz, ACT.Exp, scale=-1.0).then_inc(s_r, 1)
                if late:
                    emb_copy(g + 2, par, 2)
                if has1:
                    normed_copy(g + 1, 1 - par, i if par == 0 else i + 1)
                nc.scalar.activation(ez, zsq, ACT.Exp, scale=-0.5).then_inc(s_e, 1)

            def memory(i, first, last):
                slot(2 * i, 0, i, first, first, True, not last)
                slot(2 * i + 1, 1, i, False, first, not last, not last)
            in_pairs(act, memory)

            pq = [pz, pa]

            def queries_gelu(g, par):
                act.wait_ge(s_q, g + 1)
                wait(act, s_h1, g - 1)
                nc.scalar.activation(act2[par], pq[par][:], ACT.Gelu).then_inc(s_a2, 1)

            queries_gelu(0, 0)

            def recall(i, first, last):
                queries_gelu(2 * i + 1, 1)
                if not last:
                    queries_gelu(2 * i + 2, 0)
            in_pairs(act, recall)
            act.wait_ge(s_f, 48)
            for c in range(WPARTS):
                C = slice(c * WCOLS, (c + 1) * WCOLS)
                nc.scalar.copy(up_h[:, C], up_w[:, C]).then_inc(s_wh, 1)
            act.wait_ge(s_top, 1)
            nc.scalar.activation(ex, den, ACT.Exp).then_inc(s_rtact, 1)

            for q in range(NT // PART):
                act.wait_ge(s_oha, q + 1)
                for j in range(q * PART, (q + 1) * PART):
                    ins = nc.scalar.mul(val_a[:, j, 0, :], oh_a[:, j, :], float(j))
                ins.then_inc(s_val, 1)

            nc.scalar.activation(gelu_zero[:], tiny_c[:], ACT.Gelu)
            act.wait_ge(s_table, 1)

            def norm_rows(a, k, turn):
                act.wait_ge(s_got[k], 16 * (turn + 1))
                wait(act, s_xgT, a - 1)
                nc.scalar.activation(xg[k % 2], got[k][:, 0:D], ACT.Identity, bias=got[k][:, NMR:NMR + 1],
                                     scale=got[k][:, RSTD:RSTD + 1]).then_inc(s_xg, 1)

            norm_rows(0, 0, 0)
            norm_rows(1, 1, 0)

            def experts(i, first, last):
                for k in range(RING):
                    a = RING * i + k
                    if last and a >= NS:
                        continue
                    if not (last and a + 2 >= NS):
                        norm_rows(a + 2, (k + 2) % RING, i + (k + 2) // RING)
                    act.wait_ge(s_u, 2 * a + 1)
                    wait(act, s_hid, a - 1)
                    nc.scalar.copy(u1s[k % 2], (pz, pa)[k % 2][:, 0:F]).then_inc(s_u1, 1)
                    act.wait_ge(s_hid, a + 1)
                    wait(act, s_eaT, a - 1)
                    nc.scalar.activation(act_e[k % 2], hid[k % 2], ACT.Gelu).then_inc(s_ea, 1)
            in_rings(act, experts)

        @block.vector
        def _(dve):
            v = nc.vector
            steps = {}

            def link(ins, s):
                steps[s] = steps.get(s, 0) + 1
                ins.then_inc(s, 1)
                dve.wait_ge(s, steps[s])

            dve.wait_ge(s_pool0, 2)
            v.tensor_scalar(ident[:], colf[:], rowf[:], None, ALU.is_equal)
            v.tensor_scalar(before[:], colf[:], rowf[:], -1.0, ALU.is_gt, ALU.add)
            v.tensor_scalar(iota_m[:], colf[:, 0:E], -float(E), None, ALU.add)
            v.tensor_scalar(lastp[:], rowf[:], float(P - 1), None, ALU.is_equal)
            v.memset(ones_bf[:], 1.0)
            v.tensor_copy(colb[:], colf[:])
            v.memset(tiny_c[:], TINY)
            v.tensor_scalar(rowp1[:], rowf[:], 1.0, None, ALU.add)
            for h in range(GPS):
                for t in range(GT):
                    for half in range(2):
                        c = (h * GT + t) * (P // CHUNK) + half
                        v.memset(decay[half * CHUNK:(half + 1) * CHUNK, h, t:t + 1], GRAD * DECAY ** (NCHUNK - 1 - c))
            v.memset(rows[:, :, HB + SCORE + 1:ROW], 0.0)
            v.memset(ones_w, 1.0)
            v.memset(minus_half[:], -0.5)
            for par in range(2):
                for n in range(NGRAM):
                    lo, hi = (0, 2 if n == 2 else 1) if par == 0 else (GTOK - 1, GTOK)
                    if par == 0 or n > 0:
                        ins = v.memset(embF[par][:, n, lo:hi], 0.0)
            ins.then_inc(s_const, 1)

            def mod(dst, src, done=s_hstep):
                link(v.tensor_scalar(qi, src, 1.0 / VOCAB, None, ALU.mult), s_hstep)
                link(v.scalar_tensor_tensor(rr, qi, -float(VOCAB), src, ALU.mult, ALU.add), s_hstep)
                link(v.tensor_scalar(tt, rr, 0.0, float(VOCAB), ALU.is_lt, ALU.mult), s_hstep)
                link(v.tensor_tensor(rr, rr, tt, ALU.add), s_hstep)
                link(v.tensor_scalar(tt, rr, float(VOCAB), -float(VOCAB), ALU.is_ge, ALU.mult), s_hstep)
                link(v.tensor_tensor(dst, rr, tt, ALU.add), done)

            dve.wait_ge(s_x, 48)
            link(v.tensor_copy(hb, xw), s_hstep)
            prev = hb
            for n, cur in enumerate((h2, h3, h4)):
                link(v.tensor_copy(vv[:, 0:1], prev[:, 0:1]), s_hstep)
                link(v.scalar_tensor_tensor(vv[:, 1:HW], prev[:, 0:HW - 1], 64.0, hb[:, 1:HW], ALU.mult, ALU.add), s_hstep)
                mod(cur, vv, s_hash[n])
                prev = cur

            def newton(var, n, g, s):
                k = [0]
                ve_, se, ya_, yb_, r_ = (t[:, 0:n] for t in (ve, seed, ya, yb, rstd))

                def step(ins):
                    k[0] += 1
                    ins.then_inc(s, 1)
                    dve.wait_ge(s, g * NSTEP + k[0])
                step(v.tensor_scalar(ve_, var, EPS, None, ALU.add))
                step(v.tensor_scalar(se.bitcast(i32), ve_.bitcast(i32), 1, None, ALU.arith_shift_right))
                step(v.tensor_scalar(r_.bitcast(i32), se.bitcast(i32), -1.0, MAGIC, ALU.mult, ALU.add))
                for r in range(3):
                    step(v.scalar_tensor_tensor(ya_, r_, -0.5, ve_, ALU.mult, ALU.mult))
                    step(v.tensor_tensor(yb_, ya_, r_, ALU.mult))
                    step(v.scalar_tensor_tensor(r_, yb_, 1.5, r_, ALU.add, ALU.mult))
                assert k[0] == NSTEP

            def bn(g, s_in, s_a, s_b, at_=0):
                alone(dve, s_in, g + 1)
                for t in range(GT):
                    ins = v.bn_stats(stats[:, t, :], rowsf[:, bass.ds((g * GT + t) * ROW + HB, D)])
                ins.then_inc(s_a, 1)
                alone(dve, s_a, g + 1)
                for t in range(GT):
                    ins = v.bn_aggr(mv[:, at_ + t, :], stats[:, t, :])
                ins.then_inc(s_b, 1)
                dve.wait_ge(s_b, g + 1)

            def emb_copy(g, par):
                lo, hi = (1, GTOK) if par == 0 else (0, GTOK - 1)
                dve.wait_ge(s_eT[1], g + 1)
                wait(dve, s_h0, g - 1)
                v.tensor_copy(embF[par][:, 1, lo:hi], pe_[(NGRAM * par + 1) % 2][:, lo:hi]).then_inc(s_eF[1], 1)

            def h0_rows(g, par):
                dve.wait_ge(s_h0, g + 1)
                n = GT - 1
                v.tensor_tensor(rows[:, bass.ds(g * GT, n), 0:EXT], ph[:, 0:n * EXT].rearrange("p (t d) -> p t d", t=n),
                                bias_bc[:].unsqueeze(1).to_broadcast([P, n, EXT]), ALU.add)
                v.tensor_tensor(rows[:, bass.ds(g * GT + n, 1), 0:EXT], pe_[NGRAM * par % 2][:, 0:EXT].unsqueeze(1),
                                bias_bc[:].unsqueeze(1), ALU.add).then_inc(s_h0s, 1)
                bn(g, s_h0s, s_bn, s_ag)

            def norm(g, par):
                wait(dve, s_g0, g - 1)
                for t in range(GT):
                    ins = v.tensor_scalar(xnT[par][:, t, :], rowsf[:, bass.ds((g * GT + t) * ROW + HB, D)],
                                          mv[:, t, 0:1], rstd[:, t:t + 1], ALU.subtract, ALU.mult)
                ins.then_inc(s_xn, 1)

            dve.wait_ge(s_w, 16 * 9)
            emb_copy(0, 0)
            h0_rows(0, 0)
            newton(mv[:, 0:GT, 1], GT, 0, s_nw)
            norm(0, 0)
            zv = pz[:]
            halves = lambda w: w.rearrange("p (h c) -> p h c", h=2)

            def residual(g, par, h):
                dve.wait_ge(s_m, 2 * g + h + 1)
                v.tensor_tensor(res_t[:, h * H:(h + 1) * H].rearrange("p (t d) -> p t d", t=2),
                                pa[:, h * GTOK:h * GTOK + H].rearrange("p (t d) -> p t d", t=2),
                                decay[:, par, 2 * h:2 * h + 2].unsqueeze(2).to_broadcast([P, 2, D]), ALU.mult).then_inc(s_res, 1)

            def slot(g, par, is_first, has1, has2):
                if is_first:
                    emb_copy(1, 1)
                elif has1:
                    h0_rows(g + 1, 1 - par)
                dve.wait_ge(s_act, g + 1)
                wait(dve, s_dz, g)
                v.tensor_tensor(num, act_t, zv, ALU.mult).then_inc(s_n1, 1)
                if is_first:
                    h0_rows(1, 1)
                if has1 and not is_first:
                    newton(mv[:, 0:GT, 1], GT, g + 1, s_nw)
                wait(dve, s_rT, 2 * g)
                wait(dve, s_g1, g)
                residual(g, par, 0)
                residual(g, par, 1)
                if is_first:
                    newton(mv[:, 0:GT, 1], GT, g + 1, s_nw)
                if has1:
                    norm(g + 1, 1 - par)
                dve.wait_ge(s_rT, 2 * g + 2)
                wait(dve, s_da, g)
                v.tensor_copy(halves(res_f[:]), halves(pa[:])[:, :, H:2 * H]).then_inc(s_rF, 1)
                if has2:
                    emb_copy(g + 2, par)
                dve.wait_ge(s_n1, g + 1)
                dve.wait_ge(s_r, g + 1)
                v.scalar_tensor_tensor(num, num, TINY / 2, rz2, ALU.add, ALU.mult).then_inc(s_n2, 1)
                dve.wait_ge(s_e, g + 1)
                v.tensor_tensor(ez, ez, zv, ALU.mult).then_inc(s_n3, 1)
                dve.wait_ge(s_n2, g + 1)
                dve.wait_ge(s_n3, g + 1)
                v.scalar_tensor_tensor(num, ez, 1.0 / math.sqrt(2 * math.pi), num, ALU.mult, ALU.add).then_inc(s_gp, 1)
                dve.wait_ge(s_gp, g + 1)
                dve.wait_ge(s_da, g + 1)
                wait(dve, s_g0, g)
                v.tensor_tensor(dz, num, pa[:], ALU.mult).then_inc(s_dz, 1)

            def memory(i, first, last):
                slot(2 * i, 0, first, True, not last)
                slot(2 * i + 1, 1, False, not last, not last)
            in_pairs(dve, memory)

            dve.wait_ge(s_g0, NG)
            dve.wait_ge(s_g1, NG)
            v.tensor_copy(g0raw[:], pg[:, 0:H]).then_inc(s_ups, 1)
            v.scalar_tensor_tensor(fw1T[:], w1T[:], 1.0 - ALPHA, pg[:, H:2 * H], ALU.mult, ALU.add).then_inc(s_ups, 1)
            dve.wait_ge(s_up, 1)
            v.scalar_tensor_tensor(fw0[:], w0_s[:], 1.0 - ALPHA, ph[:, 0:H], ALU.mult, ALU.add).then_inc(s_ups, 1)
            dve.wait_ge(s_up, 2)
            v.tensor_copy(fw1[:, :, HB:EXT], pe_[0][:, 0:H].rearrange("p (c d) -> p c d", c=2)).then_inc(s_ups, 1)
            v.tensor_copy(fw1[:, :, 0:E], pe_[0][:, H:H + 2 * E].rearrange("p (c e) -> p c e", c=2)).then_inc(s_ups, 1)
            dve.wait_ge(s_up, 3)
            v.tensor_copy(wqz[:], pe_[1][:, 0:H]).then_inc(s_ups, 1)

            def recall(i, first, last):
                for par in range(2):
                    g = 2 * i + par
                    dve.wait_ge(s_h1, g + 1)
                    for h, bank in enumerate((ph, pg)):
                        here = rows[:, bass.ds(g * GT + 2 * h, 2), 0:EXT]
                        ins = v.tensor_tensor(here, bank[:, 0:2 * EXT].rearrange("p (t d) -> p t d", t=2), here, ALU.add)
                    ins.then_inc(s_h1s, 1)
                    if par == 0 and not first:
                        alone(dve, s_mvu, 2 * i)
                    bn(g, s_h1s, s_bn2, s_ag2, par * GT)
            in_pairs(dve, recall)

            rt = lambda ins: link(ins, s_rt)

            def red(dst, src, op):
                return v.tensor_reduce(dst, src, AX, op)

            def top_two(J, counts):
                n = J.stop - J.start
                b3 = lambda a: a.unsqueeze(2).to_broadcast([P, n, E])
                iota = iota_m[:].unsqueeze(1).to_broadcast([P, n, E])
                lg = logits[:, J, :]
                for c, m in ((0, m1), (1, m2)):
                    t, oh = t01[:, J, c], oh01[:, J, c, :]
                    rt(red(m[:, J], lg, ALU.max))
                    rt(v.tensor_tensor(eqm[:, J, :], lg, b3(m[:, J]), ALU.is_equal))
                    rt(v.tensor_tensor(cand[:, J, :], eqm[:, J, :], iota, ALU.mult))
                    rt(red(t, cand[:, J, :], ALU.min))
                    rt(v.tensor_tensor(oh, cand[:, J, :], b3(t), ALU.is_equal))
                    if c == 0:
                        rt(v.scalar_tensor_tensor(lg2[:, J, :], oh, -BIG, lg, ALU.mult, ALU.add))
                        lg = lg2[:, J, :]
                rt(red(counts, oh01[:, J, :, :].rearrange("p j v e -> p (v e) j"), ALU.add))

            early = (NG - 2) * GT
            dve.wait_ge(s_lgs, NG // 2 - 1)
            top_two(slice(0, early), cnt_a)
            rt(v.memset(ones_f, 1.0))
            dve.wait_ge(s_lgs, NG // 2)
            top_two(slice(early, NT), cnt_b)
            link(v.tensor_tensor(cnt, cnt_a, cnt_b, ALU.add), s_cready)
            link(v.tensor_tensor(den, m2, m1, ALU.subtract), s_top)
            rt(v.tensor_tensor(imax, t01[:, :, 0], t01[:, :, 1], ALU.max))
            L = slice(NT - 1, NT)
            dve.wait_ge(s_cnt, 1)
            rt(v.tensor_scalar(full, pz[:, 0:2 * E], float(TOK), None, ALU.is_ge))
            rt(v.tensor_tensor(kk, full, oh01[:, NT - 1, :, :].rearrange("p v e -> p (v e)"), ALU.mult))
            rt(red(drop, kk.rearrange("p (v e) -> p v e", v=2), ALU.add))
            rt(v.tensor_scalar(drop, drop, lastp[:], None, ALU.mult))
            link(v.tensor_scalar(stay, drop, -1.0, 1.0, ALU.mult, ALU.add), s_stay)
            rt(v.scalar_tensor_tensor(both, t01[:, NT - 1, :], float(E), stay, ALU.add, ALU.mult))
            rt(v.tensor_tensor(imax[:, L], both[:, 0:1], both[:, 1:2], ALU.max))
            rt(v.tensor_scalar(imax[:, L], imax[:, L], -float(E), None, ALU.add))
            link(v.tensor_tensor(ohm, iota_m[:].unsqueeze(1).to_broadcast([P, NT, E]),
                                 imax.unsqueeze(2).to_broadcast([P, NT, E]), ALU.is_equal), s_ohm)
            dve.wait_ge(s_rtact, 1)
            rt(v.tensor_scalar(den, ex, 1.0, None, ALU.add))
            link(v.reciprocal(s0, den), s_s0)
            dve.wait_ge(s_rank, 1)
            tot = pa[:, 512:512 + fE].rearrange("p (j e) -> p j e", e=E)
            for e in range(E):
                ins = v.tensor_tensor_scan(incl[:, :, e], ones_f, tot[:, :, e], 0.0, ALU.mult, ALU.add)
            rt(ins)
            rt(v.tensor_scalar(nt_i, incl[:, NT - 1, :], float(P - 1), None, ALU.add))
            rt(v.tensor_scalar(nt_i, nt_i, 7, None, ALU.arith_shift_right))
            rt(v.tensor_copy(nt_f, nt_i))
            rt(v.tensor_tensor_scan(nt_c, ones_f[:, 0:E], nt_f, 0.0, ALU.mult, ALU.add))
            rt(v.tensor_tensor(first, nt_c, nt_f, ALU.subtract))
            rt(v.tensor_scalar(nt_f, first, float(P), None, ALU.mult))
            rt(v.tensor_tensor(base, incl, pa[:, 0:fE].rearrange("p (j e) -> p j e", e=E), ALU.add))
            rt(v.tensor_tensor(base, base, nt_f.unsqueeze(1).to_broadcast([P, NT, E]), ALU.add))
            rt(v.tensor_tensor(base, base, ohm, ALU.mult))
            rt(red(pos, base, ALU.add))
            rt(v.tensor_copy(pos_i, pos))
            rt(v.tensor_scalar(a_i, pos_i, 7, None, ALU.arith_shift_right))
            rt(v.tensor_scalar(b_i, pos_i, P - 1, None, ALU.bitwise_and))
            rt(v.tensor_copy(slot_a, a_i))
            rt(v.tensor_copy(slot_b, b_i))
            wb = colb[:].unsqueeze(1)
            for q in range(NT // PART):
                J = slice(q * PART, (q + 1) * PART)
                v.tensor_tensor(oh_a[:, J, :], wb[:, :, 0:NSP].to_broadcast([P, PART, NSP]),
                                slot_a[:, J].unsqueeze(2).to_broadcast([P, PART, NSP]), ALU.is_equal).then_inc(s_oha, 1)
                v.tensor_tensor(oh_b[:, J, :], wb.to_broadcast([P, PART, P]),
                                slot_b[:, J].unsqueeze(2).to_broadcast([P, PART, P]), ALU.is_equal)
                dve.wait_ge(s_oha, q + 1)
                v.tensor_scalar(val_a[:, J, 1, :], oh_a[:, J, :], rowp1[:], None, ALU.mult).then_inc(s_onehot, 1)
            rt(v.tensor_tensor(starts, colf[:, 0:NS].unsqueeze(2).to_broadcast([P, NS, E]),
                               first.unsqueeze(1).to_broadcast([P, NS, E]), ALU.is_ge))
            rt(v.tensor_reduce(tile_e, starts, AX, ALU.add))
            rt(v.tensor_scalar(exp_idx[:, 0:NS], tile_e, -1.0, None, ALU.add))
            dve.wait_ge(s_slots, 1)
            rt(v.tensor_copy(slot_v[:], pe_[0][:, NSP:2 * NSP]))
            rt(v.scalar_tensor_tensor(slot_v[:], pe_[0][:, 0:NSP], float(P), slot_v[:], ALU.mult, ALU.add))
            rt(v.tensor_scalar(slot_idx[:, :, 0], slot_v[:], -1.0, 0.0, ALU.add, ALU.max))
            rt(v.tensor_scalar(val0[:], slot_v[:], 0.0, SKIP, ALU.is_equal, ALU.mult))
            link(v.scalar_tensor_tensor(slot_idx[:, :, 1], slot_v[:], -1.0, val0[:], ALU.add, ALU.add), s_table)

            def in_copy(a, k):
                dve.wait_ge(s_xgT, a + 1)
                wait(dve, s_u, 2 * a - 2)
                v.tensor_copy(xg_h[k % 2][:], ph[:, 0:P]).then_inc(s_xgH, 1)
                dve.wait_ge(s_xgH, a + 1)
                v.tensor_tensor(xg_l[k % 2][:], ph[:, 0:P], xg_h[k % 2][:].bitcast(f32), ALU.subtract).then_inc(s_xgF, 1)

            def gelu_copy(a, k):
                dve.wait_ge(s_eaT, a + 1)
                wait(dve, s_y, a - 1)
                v.tensor_copy(act_eF[k % 2], pe_[0][:]).then_inc(s_eaF, 1)

            def out_rows(a, k, i):
                dve.wait_ge(s_y, a + 1)
                if isinstance(a, int):
                    wait(dve, s_put[k % 2], 16 * ((a - 2) // 2 + 1))
                else:
                    dve.wait_ge(s_put[k % 2], 16 * (i * (RING // 2) + (k - 2) // 2 + 1))
                r = got[k % RING]
                v.scalar_tensor_tensor(outs[k % 2], pe_[1][:, 0:D], r[:, SCORE:SCORE + 1], r[:, 0:D],
                                       ALU.mult, ALU.add).then_inc(s_o, 1)

            in_copy(0, 0)
            in_copy(1, 1)

            def experts(i, first_, last_):
                for k in range(RING):
                    a = RING * i + k
                    if not (last_ and a >= NS):
                        dve.wait_ge(s_u, 2 * a + 2)
                        dve.wait_ge(s_u1, a + 1)
                        wait(dve, s_ea, a - 1)
                        v.tensor_tensor(hid[k % 2], u1s[k % 2], (pz, pa)[k % 2][:, F:2 * F], ALU.mult).then_inc(s_hid, 1)
                    if not (first_ and k < 1) and not (last_ and a - 1 >= NS):
                        gelu_copy(a - 1, k - 1)
                    if not (last_ and a + 2 >= NS):
                        in_copy(a + 2, k + 2)
                    if not (first_ and k < 2) and not (last_ and a - 2 >= NS):
                        out_rows(a - 2, k - 2, i)
            in_rings(dve, experts)
            n = (NS + RING - 1) // RING
            for a in range(n * RING - 2, NS):
                out_rows(a, a % RING, 0)

        @block.tensor
        def _(pe):
            mm, tr = nc.tensor.matmul, nc.tensor.transpose
            pe.wait_ge(s_const, 1)
            hT = (pg, pe_[0], pe_[1])

            def keep_clock(n, to=pa[:, GTOK:GTOK + NGRAM * D]):
                for _ in range(n):
                    mm(to, ident[:], proj_s[:], start=True, stop=True)

            def hash_T(n, h):
                pe.wait_ge(s_hash[n], 1)
                tr(hT[n][:, 0:NT], h, ident[0:NT, 0:NT]).then_inc(s_hT, 1)

            hash_T(0, h2[:, 2:2 + P])
            pe.wait_ge(s_w, 16 * 9)
            for n in range(NGRAM):
                tr(pz[:, n * D:(n + 1) * D], proj_s[:, n * D:(n + 1) * D], ident[:])
            hash_T(1, h3[:, 3:3 + P])
            tr(pa[:, 0:D], wk_s[:], ident[:])
            tr(pa[:, D:2 * D], wq_s[:], ident[:])
            tr(pa[:, 2 * D:3 * D], w1_s[:, 0, :], ident[:])
            tr(pa[:, 3 * D:4 * D], w1_s[:, 1, :], ident[:])
            tr(pa[:, GTOK:GTOK + P], bias_bc[:, HB:EXT], ident[:])
            for n in range(NGRAM):
                at_ = NGRAM * D + n * E
                ins = mm(pz[:, at_:at_ + E], proj_s[:, n * D:(n + 1) * D], wr_s[:], start=True, stop=True)
            ins.then_inc(s_wT, 1)
            hash_T(2, h4[:, 3:3 + P])
            pe.wait_ge(s_wTs, 7)
            mm(ph[:, 0:H], wkT[:], w0_s[:], start=True, stop=True)
            mm(ph[:, H:H + E], biasT, wr_s[:], start=True, stop=True)
            mm(ph[:, H + E:H + 2 * E], ones_w, wr_s[:], start=True, stop=True).then_inc(s_wkz, 1)
            pe.wait_ge(s_idx, NGRAM)
            pe.wait_ge(s_wkzs, 1)

            def emb_T(g, par, i, which=range(NGRAM)):
                for n in which:
                    pe.wait_ge(s_gath[par][n], 16 * GT * (i + 1))
                    wait(pe, s_eF[(n + 1) % NGRAM], g if n < 2 else g + 1)
                    if n == 1:
                        wait(pe, s_h0s, g)
                    for t in range(GT):
                        ins = tr(pe_[(NGRAM * par + n) % 2][:, t * P:(t + 1) * P], gath[par][:, n, t, :], ident[:])
                    ins.then_inc(s_eT[n], 1)

            def h0_early():
                for n in range(NGRAM - 1):
                    pe.wait_ge(s_eF[n], 1)
                    for t in range(GT - 1):
                        mm(ph[:, t * EXT:(t + 1) * EXT], embF[0][:, n, t * P:(t + 1) * P], projT[:, n, :],
                           start=(n == 0 and t == 0), stop=False, skip_group_check=True)

            def h0_late():
                pe.wait_ge(s_eF[NGRAM - 1], 1)
                n = NGRAM - 1
                for t in range(GT - 1):
                    mm(ph[:, t * EXT:(t + 1) * EXT], embF[0][:, n, t * P:(t + 1) * P], projT[:, n, :],
                       start=False, stop=True, skip_group_check=True)
                h0_mm(0, 0, [GT - 1])

            def h0_mm(g, par, tiles=range(GT)):
                for n in range(NGRAM):
                    pe.wait_ge(s_eF[n], g + 1)
                wait(pe, s_xF, g)
                for t in tiles:
                    to = ph[:, t * EXT:(t + 1) * EXT] if t < GT - 1 else pe_[NGRAM * par % 2][:, 0:EXT]
                    for n in range(NGRAM):
                        ins = mm(to, embF[par][:, n, t * P:(t + 1) * P], projT[:, n, :],
                                 start=(n == 0), stop=(n == NGRAM - 1))
                ins.then_inc(s_h0, 1)

            def xn_T(g, par):
                pe.wait_ge(s_xn, g + 1)
                for t in range(GT):
                    ins = tr(ph[:, t * P:(t + 1) * P], xnT[par][:, t, :], ident[:])
                ins.then_inc(s_xT, 1)

            def grad0(g, par, tiles):
                pe.wait_ge(s_dz, g + 1)
                for t in tiles:
                    ins = mm(pg[:, 0:H], xnT[par][:, t, :], dz[:, t * H:(t + 1) * H],
                             start=False, stop=False, skip_group_check=True)
                if t == GT - 1:
                    ins.then_inc(s_g0, 1)

            emb_T(0, 0, 0, [0])
            keep_clock(1)
            emb_T(0, 0, 0, [1])
            h0_early()
            keep_clock(2)
            emb_T(0, 0, 0, [2])
            keep_clock(1)
            h0_late()
            keep_clock(7)
            xn_T(0, 0)

            def slot(g, par, i, is_first, late, has1, has2):
                pe.wait_ge(s_xF, g + 1)
                wait(pe, s_n3, g)
                for t in range(GT):
                    ins = mm(pz[:, t * H:(t + 1) * H], xnF[par][:, t * P:(t + 1) * P], wkz[:], start=True, stop=True)
                ins.then_inc(s_z, 1)
                if is_first:
                    emb_T(1, 1, 0, (0, 1))
                if has2 and not late:
                    emb_T(g + 2, par, i + 1, (0, 1))
                if not is_first:
                    grad0(g - 1, 1 - par, (0, 1))
                pe.wait_ge(s_act, g + 1)
                for c in range(2):
                    for t in range(GT):
                        ins = tr(pa[:, c * GTOK + t * P:c * GTOK + (t + 1) * P], act_t[:, t * H + c * P:t * H + (c + 1) * P], ident[:])
                ins.then_inc(s_aT, 1)
                if is_first:
                    emb_T(1, 1, 0, (2,))
                    h0_mm(1, 1)
                if not is_first:
                    grad0(g - 1, 1 - par, (2, 3))
                if has2 and not late:
                    emb_T(g + 2, par, i + 1, (2,))
                pe.wait_ge(s_aF, g + 1)
                for h in range(2):
                    for t in (2 * h, 2 * h + 1):
                        T = slice(t * P, (t + 1) * P)
                        to = pa[:, h * GTOK + (t - 2 * h) * P:h * GTOK + (t - 2 * h + 1) * P]
                        mm(to, act_f[:, T], w1_s[:, 0, :], start=True, stop=False)
                        mm(to, act_f[:, GTOK + t * P:GTOK + (t + 1) * P], w1_s[:, 1, :], start=False, stop=False)
                        ins = mm(to, xnF[par][:, T], nwv[:], start=False, stop=True)
                    ins.then_inc(s_m, 1)
                if late:
                    emb_T(g + 2, par, i + 1, (0, 1))
                for h in range(2):
                    pe.wait_ge(s_res, 2 * g + h + 1)
                    for t in (2 * h, 2 * h + 1):
                        to = h * GTOK + H + (t - 2 * h) * P
                        ins = tr(pa[:, to:to + P], res_t[:, t * P:(t + 1) * P], ident[:])
                    ins.then_inc(s_rT, 1)
                    for t in (2 * h, 2 * h + 1):
                        one = is_first and t == 0
                        ins = mm(pg[:, H:2 * H], res_t[:, t * P:(t + 1) * P], act_t[:, t * H:(t + 1) * H],
                                 start=one, stop=False, skip_group_check=True)
                ins.then_inc(s_g1, 1)
                if late:
                    emb_T(g + 2, par, i + 1, (2,))
                if has1:
                    xn_T(g + 1, 1 - par)
                pe.wait_ge(s_rF, g + 1)
                for t in range(GT):
                    ins = mm(pa[:, t * H:(t + 1) * H], res_f[:, t * P:(t + 1) * P], w1T[:], start=True, stop=True)
                ins.then_inc(s_da, 1)
                if has2:
                    h0_mm(g + 2, par)

            def memory(i, first, last):
                slot(2 * i, 0, i, first, first, True, not last)
                slot(2 * i + 1, 1, i, False, first, not last, not last)
            in_pairs(pe, memory)
            keep_clock(4, ph[:, 0:NGRAM * D])
            grad0(NG - 1, 1, range(GT))

            pe.wait_ge(s_ups, 2)
            mm(ph[:, 0:H], wk_s[:], g0raw[:], start=True, stop=True).then_inc(s_up, 1)
            tr(pe_[0][:, 0:D], fw1T[:, 0:D], ident[:])
            tr(pe_[0][:, D:H], fw1T[:, D:H], ident[:])
            for c in range(2):
                ins = mm(pe_[0][:, H + c * E:H + (c + 1) * E], fw1T[:, c * P:(c + 1) * P], wr_s[:], start=True, stop=True)
            ins.then_inc(s_up, 1)
            pe.wait_ge(s_ups, 3)
            mm(pe_[1][:, 0:H], wqT[:], fw0[:], start=True, stop=True).then_inc(s_up, 1)
            pe.wait_ge(s_ups, 6)
            for par in range(2):
                pe.wait_ge(s_xall[par], 16 * (NG // 2))

            pq = [pz, pa]

            def query(g, par):
                wait(pe, s_a2, g - 1)
                for c in range(2):
                    ins = mm(pq[par][:, c * GTOK:(c + 1) * GTOK], wqz[:, c * P:(c + 1) * P],
                             xnF_all[:, bass.ds(g * GTOK, GTOK)], start=True, stop=True)
                ins.then_inc(s_q, 1)

            def h1_mm(g, par):
                pe.wait_ge(s_a2, g + 1)
                wait(pe, s_h1s, g)
                for t in range(GT):
                    to = (ph, pg)[t // 2][:, (t % 2) * EXT:(t % 2 + 1) * EXT]
                    for c in range(2):
                        ins = mm(to, act2[par][:, c * GTOK + t * P:c * GTOK + (t + 1) * P],
                                 fw1[:, c, :], start=(c == 0), stop=(c == 1))
                ins.then_inc(s_h1, 1)

            query(0, 0)

            def recall(i, first, last):
                query(2 * i + 1, 1)
                h1_mm(2 * i, 0)
                if not last:
                    query(2 * i + 2, 0)
                h1_mm(2 * i + 1, 1)
            in_pairs(pe, recall)

            pe.wait_ge(s_cready, 1)
            mm(pz[:, 0:E], ones_bf[:], cnt[:, 0:E], start=True, stop=True)
            mm(pz[:, E:2 * E], ones_bf[:], cnt[:, 0:E], start=True, stop=False)
            mm(pz[:, E:2 * E], ones_bf[:], cnt[:, E:2 * E], start=False, stop=True).then_inc(s_cnt, 1)
            pe.wait_ge(s_ohm, 1)
            mm(pa[:, 512:512 + fE], ones_bf[:], ohm, start=True, stop=True)
            mm(pa[:, 0:fE], before[:], ohm, start=True, stop=True).then_inc(s_rank, 1)
            for j in range(NT):
                if j % PART == 0:
                    pe.wait_ge(s_onehot, j // PART + 1)
                    pe.wait_ge(s_val, j // PART + 1)
                ins = mm(pe_[0][:, 0:2 * NSP], oh_b[:, j, :], val_a[:, j, :, :].rearrange("p v a -> p (v a)"),
                         start=(j == 0), stop=(j == NT - 1))
                if j % PART == PART - 1 and j < NT - 1:
                    keep_clock(2)
            ins.then_inc(s_slots, 1)

            keep_clock(8)
            pe.wait_ge(s_wl, WPARTS)
            pe.wait_ge(s_table, 1)

            def in_T(a, k):
                pe.wait_ge(s_xg, a + 1)
                wait(pe, s_xgF, a)
                tr(ph[:, 0:P], xg[k % 2], ident[:]).then_inc(s_xgT, 1)

            def expert_of(a):
                return pe.value_load(exp_idx[0:1, bass.ds(a, 1)], min_val=0, max_val=E - 1)

            def down(a, k, e):
                pe.wait_ge(s_eaF, a + 1)
                wait(pe, s_o, a)
                for c in range(4):
                    ins = mm(pe_[1][:, 0:D], act_eF[k % 2][:, c * P:(c + 1) * P], f3_f[:, bass.ds(e * F + c * D, D)],
                             start=(c == 0), stop=(c == 3))
                ins.then_inc(s_y, 1)

            def gelu_T(a, k):
                pe.wait_ge(s_ea, a + 1)
                wait(pe, s_eaF, a)
                for c in range(4):
                    ins = tr(pe_[0][:, c * P:(c + 1) * P], act_e[k % 2][:, c * P:(c + 1) * P], ident[:])
                ins.then_inc(s_eaT, 1)

            in_T(0, 0)
            in_T(1, 1)

            def experts(i, first, last):
                e = {0: expert_of(0)} if first else {
                    k: nc.snap(behind[k], engines=[mybir.EngineType.PE], min_val=0, max_val=E - 1) for k in (-2, -1, 0)}
                for k in range(RING):
                    a = RING * i + k
                    if not (last and a >= NS):
                        pu = (pz, pa)[k % 2]
                        pe.wait_ge(s_xgF, a + 1)
                        wait(pe, s_hid, a - 1)
                        x_h, x_l = xg_h[k % 2][:], xg_l[k % 2][:]
                        for h in range(2):
                            W = bass.ds(e[k] * F + h * E * F, F)
                            to = pu[:, h * F:(h + 1) * F]
                            mm(to, x_h, up_h[:, W], start=True, stop=False)
                            mm(to, x_h, up_l[:, W], start=False, stop=False)
                            mm(to, x_l, up_h[:, W], start=False, stop=True).then_inc(s_u, 1)
                    if not (last and a + 1 >= NS):
                        e[k + 1] = expert_of(a + 1)
                    if not (last and a + 2 >= NS):
                        in_T(a + 2, k + 2)
                    if not (first and k < 1) and not (last and a - 1 >= NS):
                        gelu_T(a - 1, k - 1)
                    if not (first and k < 2) and not (last and a - 2 >= NS):
                        down(a - 2, k - 2, e[k - 2])
                if not last:
                    for k in behind:
                        pe.reg_mov(behind[k], e[RING + k])
            behind = {-2: pe.alloc_register("expert_of_last_but_one"), -1: pe.alloc_register("expert_of_last"),
                      0: pe.alloc_register("expert_of_next")}
            in_rings(pe, experts)
            n = (NS + RING - 1) // RING
            for a in range(n * RING - 2, NS):
                down(a, a, expert_of(a))


_INS = ['x', 'L0_tok_emb_2', 'L0_tok_emb_3', 'L0_tok_emb_4', 'L0_tok_proj_w', 'L0_tok_proj_b', 'L0_attn_w_k',
        'L0_attn_w_v', 'L0_attn_w_q', 'L0_attn_W0', 'L0_attn_W1', 'L0_ffn_Wr', 'L0_ffn_br', 'L0_ffn_W1',
        'L0_ffn_W2', 'L0_ffn_W3']
_OUTS = [((BATCH, SEQ, D), 'float32')]


def kernel(**inputs):
    import numpy as _np
    import concourse.bacc as _bacc
    from concourse import mybir as _mybir
    from concourse.bass_utils import run_bass_kernel_spmd as _run

    nc = _bacc.Bacc("TRN2", target_bir_lowering=False, num_devices=1)
    arrays, args = {}, []
    for name in _INS:
        a = _np.ascontiguousarray(inputs[name])
        arrays[f"in_{name}_dram"] = a
        args.append(nc.dram_tensor(f"in_{name}_dram", a.shape, _mybir.dt.from_np(a.dtype), kind="ExternalInput").ap())
    for i, (shape, dtype) in enumerate(_OUTS):
        dt = _mybir.dt.from_np(_np.dtype(dtype))
        args.append(nc.dram_tensor(f"out_{i}_dram", shape, dt, kind="ExternalOutput").ap())
    tower(nc, *args)
    r = _run(nc, [arrays], core_ids=[0])
    return r.results[0]["out_0_dram"]
```
